# Optimizing a Trainium2 kernel written in Bass

```python
import numpy as np
import jax
import jax.numpy as jnp

def _softmax(x, axis=-1):
    return jax.nn.softmax(x, axis=axis)

def _gelu(x):
    return jax.nn.gelu(x, approximate=True)

def _silu(x):
    return jax.nn.silu(x)

def _sigmoid(x):
    return jax.nn.sigmoid(x)

def _layernorm(x, axis=-1, eps=1e-05):
    m = jnp.mean(x, axis=axis, keepdims=True)
    v = jnp.var(x, axis=axis, keepdims=True)
    return (x - m) / jnp.sqrt(v + eps)

def _scatter_add(tgt, idx, src, axis=0):
    return tgt.at[idx].add(src)

def _segment_sum(src, seg, n):
    return jax.ops.segment_sum(src, seg, n)
kernel_name = 'mk_lm_tower_d1_tok_ids512_r4_daef8a'

def setup_inputs(seed: int=0):
    np.random.seed(seed)
    _w = jnp.asarray

    def _rec_inputs():
        import jax
        import jax.numpy as jnp
        _rk = jax.random.key(seed)
        x = jax.random.randint(jax.random.fold_in(_rk, 1), (8, 512), 0, 24991, jnp.int32)
        return x
    x = _rec_inputs()

    def _L0_tok_setup():
        import jax, jax.numpy as jnp
        import numpy as np
        VOCAB = 25000
        HIDDEN = 128
        NUM_CLUSTERS = 64
        B, S = (8, 512)
        key = jax.random.key(seed)
        k1, k2, k3, k4, k5 = jax.random.split(key, 5)
        return {'location_ids': jax.random.randint(k1, (B, S), 0, VOCAB), 'fine_embed_w': jax.random.normal(k2, (VOCAB, HIDDEN // 2), dtype=jnp.float32), 'coarse_embed_w': jax.random.normal(k3, (NUM_CLUSTERS, HIDDEN // 2), dtype=jnp.float32), 'loc_to_cluster_w': jax.random.normal(k4, (NUM_CLUSTERS, VOCAB), dtype=jnp.float32), 'loc_to_cluster_b': jax.random.normal(k5, (NUM_CLUSTERS,), dtype=jnp.float32)}
    _L0_tok_all = _L0_tok_setup()
    _L0_tok_in = {k: v for k, v in _L0_tok_all.items() if k in ('fine_embed_w', 'coarse_embed_w', 'loc_to_cluster_w', 'loc_to_cluster_b')}
    del _L0_tok_all

    def _L0_attn_setup():
        import jax, jax.numpy as jnp
        import numpy as np
        EPS = 1.1920929e-07

        def _rms_norm(x):
            return x * jax.lax.rsqrt(jnp.mean(jnp.square(x), axis=-1, keepdims=True) + EPS)
        key = jax.random.key(seed)
        ks = jax.random.split(key, 10)
        B, T, V, C, NB = (4, 1024, 128, 128, 64)
        s = 0.02
        return {'x': jax.random.normal(ks[0], (B, T, V), dtype=jnp.float32), 'basis': jax.random.normal(ks[1], (V, 2 * NB), dtype=jnp.float32), 'q_coeffs': jax.random.normal(ks[2], (C, 2 * NB), dtype=jnp.float32) * s, 'k_coeffs': jax.random.normal(ks[3], (C, 2 * NB), dtype=jnp.float32) * s, 'v_coeffs': jax.random.normal(ks[4], (C, 2 * NB), dtype=jnp.float32) * s, 'o_coeffs': jax.random.normal(ks[5], (C, 2 * NB), dtype=jnp.float32) * s, 'decay_logit': jnp.float32(3.0), 'mem_out_scale': jnp.float32(0.1), 'read_coeffs': jax.random.normal(ks[6], (C, 2 * NB), dtype=jnp.float32) * s, 'write_coeffs': jax.random.normal(ks[7], (C, 2 * NB), dtype=jnp.float32) * s, 'channel_mix': jax.random.normal(ks[8], (C, C), dtype=jnp.float32) * s, 'bias': jnp.zeros((C,), dtype=jnp.float32), 'op_out_scale': jnp.float32(0.1), 'mem_scale': jnp.ones((1,), dtype=jnp.float32), 'op_scale': jnp.ones((1,), dtype=jnp.float32)}
    _L0_attn_all = _L0_attn_setup()
    _L0_attn_in = {k: v for k, v in _L0_attn_all.items() if k in ('basis', 'q_coeffs', 'k_coeffs', 'v_coeffs', 'o_coeffs', 'decay_logit', 'mem_out_scale', 'read_coeffs', 'write_coeffs', 'channel_mix', 'bias', 'op_out_scale', 'mem_scale', 'op_scale')}
    del _L0_attn_all

    def _L0_ffn_setup():
        import jax, jax.numpy as jnp
        import numpy as np
        TOP_K = 6
        CAP_FACTOR = 2.0
        key = jax.random.key(seed)
        ks = jax.random.split(key, 9)
        B, S, D, F, E, SH = (4, 512, 128, 64, 64, 2)
        return {'x': jax.random.normal(ks[0], (B, S, D), jnp.float32), 'router_w': jax.random.normal(ks[1], (E, D), jnp.float32) * 0.02, 'bias': jnp.zeros((E,), jnp.float32), 'shared_w_gate': jax.random.normal(ks[2], (SH, F, D), jnp.float32) * 0.02, 'shared_w_up': jax.random.normal(ks[3], (SH, F, D), jnp.float32) * 0.02, 'shared_w_down': jax.random.normal(ks[4], (SH, D, F), jnp.float32) * 0.02, 'w_gate': jax.random.normal(ks[5], (E, F, D), jnp.float32) * 0.02, 'w_up': jax.random.normal(ks[6], (E, F, D), jnp.float32) * 0.02, 'w_down': jax.random.normal(ks[7], (E, D, F), jnp.float32) * 0.02}
    _L0_ffn_all = _L0_ffn_setup()
    _L0_ffn_in = {k: v for k, v in _L0_ffn_all.items() if k in ('router_w', 'bias', 'shared_w_gate', 'shared_w_up', 'shared_w_down', 'w_gate', 'w_up', 'w_down')}
    del _L0_ffn_all
    return {'x': x, 'L0_tok_fine_embed_w': _L0_tok_in['fine_embed_w'], 'L0_tok_coarse_embed_w': _L0_tok_in['coarse_embed_w'], 'L0_tok_loc_to_cluster_w': _L0_tok_in['loc_to_cluster_w'], 'L0_tok_loc_to_cluster_b': _L0_tok_in['loc_to_cluster_b'], 'L0_attn_basis': _L0_attn_in['basis'], 'L0_attn_q_coeffs': _L0_attn_in['q_coeffs'], 'L0_attn_k_coeffs': _L0_attn_in['k_coeffs'], 'L0_attn_v_coeffs': _L0_attn_in['v_coeffs'], 'L0_attn_o_coeffs': _L0_attn_in['o_coeffs'], 'L0_attn_decay_logit': _L0_attn_in['decay_logit'], 'L0_attn_mem_out_scale': _L0_attn_in['mem_out_scale'], 'L0_attn_read_coeffs': _L0_attn_in['read_coeffs'], 'L0_attn_write_coeffs': _L0_attn_in['write_coeffs'], 'L0_attn_channel_mix': _L0_attn_in['channel_mix'], 'L0_attn_bias': _L0_attn_in['bias'], 'L0_attn_op_out_scale': _L0_attn_in['op_out_scale'], 'L0_attn_mem_scale': _L0_attn_in['mem_scale'], 'L0_attn_op_scale': _L0_attn_in['op_scale'], 'L0_ffn_router_w': _L0_ffn_in['router_w'], 'L0_ffn_bias': _L0_ffn_in['bias'], 'L0_ffn_shared_w_gate': _L0_ffn_in['shared_w_gate'], 'L0_ffn_shared_w_up': _L0_ffn_in['shared_w_up'], 'L0_ffn_shared_w_down': _L0_ffn_in['shared_w_down'], 'L0_ffn_w_gate': _L0_ffn_in['w_gate'], 'L0_ffn_w_up': _L0_ffn_in['w_up'], 'L0_ffn_w_down': _L0_ffn_in['w_down']}

def reference(x, L0_tok_fine_embed_w, L0_tok_coarse_embed_w, L0_tok_loc_to_cluster_w, L0_tok_loc_to_cluster_b, L0_attn_basis, L0_attn_q_coeffs, L0_attn_k_coeffs, L0_attn_v_coeffs, L0_attn_o_coeffs, L0_attn_decay_logit, L0_attn_mem_out_scale, L0_attn_read_coeffs, L0_attn_write_coeffs, L0_attn_channel_mix, L0_attn_bias, L0_attn_op_out_scale, L0_attn_mem_scale, L0_attn_op_scale, L0_ffn_router_w, L0_ffn_bias, L0_ffn_shared_w_gate, L0_ffn_shared_w_up, L0_ffn_shared_w_down, L0_ffn_w_gate, L0_ffn_w_up, L0_ffn_w_down):
    import jax
    import jax.numpy as jnp

    def _L0_tok_ref(location_ids, fine_embed_w, coarse_embed_w, loc_to_cluster_w, loc_to_cluster_b):
        import jax, jax.numpy as jnp
        import numpy as np
        VOCAB = 25000
        HIDDEN = 128
        NUM_CLUSTERS = 64
        B, S = (8, 512)
        fine_emb = fine_embed_w[location_ids]
        cluster_logits = loc_to_cluster_w.T[location_ids] + loc_to_cluster_b
        cluster_dist = jax.nn.softmax(cluster_logits, axis=-1)
        coarse_emb = jnp.einsum('bsc,ch->bsh', cluster_dist, coarse_embed_w)
        return jnp.concatenate([fine_emb, coarse_emb], axis=-1)

    def _L0_attn_ref(x, basis, q_coeffs, k_coeffs, v_coeffs, o_coeffs, decay_logit, mem_out_scale, read_coeffs, write_coeffs, channel_mix, bias, op_out_scale, mem_scale, op_scale):
        import jax, jax.numpy as jnp
        import numpy as np
        EPS = 1.1920929e-07

        def _rms_norm(x):
            return x * jax.lax.rsqrt(jnp.mean(jnp.square(x), axis=-1, keepdims=True) + EPS)
        B, T, V = x.shape
        dt = x.dtype
        xn = _rms_norm(x)
        q_w = basis @ q_coeffs.T
        k_w = basis @ k_coeffs.T
        v_w = basis @ v_coeffs.T
        o_w = basis @ o_coeffs.T
        q = xn @ q_w
        k = xn @ k_w
        v = xn @ v_w
        scores = jnp.einsum('btc,bsc->bts', q, k)
        decay = jax.nn.sigmoid(decay_logit)
        pos = jnp.arange(T)
        diff = pos[None, :] - pos[:, None]
        expn = jnp.maximum(diff - 1, 0).astype(dt)
        decay_w = jnp.power(decay.astype(dt), expn) * (diff > 0).astype(dt)
        retrieved = jnp.einsum('bts,bsc->btc', scores * decay_w[None], v)
        mem_out = retrieved @ o_w.T * mem_out_scale.astype(dt)
        x = x + mem_scale.astype(dt) * mem_out
        xn2 = _rms_norm(x)
        read_w = jax.nn.softmax(basis @ read_coeffs.T, axis=0).astype(dt)
        vals = xn2 @ read_w @ channel_mix.astype(dt) + bias.astype(dt)
        vals = jax.nn.gelu(vals, approximate=False)
        write_w = (basis @ write_coeffs.T).astype(dt)
        op_out = vals @ write_w.T * op_out_scale.astype(dt)
        return x + op_scale.astype(dt) * op_out

    def _L0_ffn_ref(x, router_w, bias, shared_w_gate, shared_w_up, shared_w_down, w_gate, w_up, w_down):
        import jax, jax.numpy as jnp
        import numpy as np
        TOP_K = 6
        CAP_FACTOR = 2.0
        B, S, D = x.shape
        E = router_w.shape[0]
        K = TOP_K
        N = B * S
        C = max(1, int(N * K * CAP_FACTOR / E))
        router_logits = jnp.einsum('bsd,ed->bse', x, router_w) + bias
        hg = jnp.einsum('bsd,efd->bsef', x, shared_w_gate)
        hu = jnp.einsum('bsd,efd->bsef', x, shared_w_up)
        shared_out = jnp.einsum('bsef,edf->bsd', jax.nn.silu(hg) * hu, shared_w_down)
        shared_out = shared_out / shared_w_gate.shape[0]
        router_probs = jax.nn.softmax(router_logits, axis=-1)
        topk_p, topk_i = jax.lax.top_k(router_probs, K)
        topk_p = topk_p / (jnp.sum(topk_p, axis=-1, keepdims=True) + 1e-09)
        x_flat = x.reshape(N, D)
        flat_e = topk_i.reshape(-1)
        flat_g = topk_p.reshape(-1)
        token_ids = jnp.repeat(jnp.arange(N), K)
        order = jnp.argsort(flat_e)
        se = flat_e[order]
        st = token_ids[order]
        sg = flat_g[order]
        M = se.shape[0]
        pos = jnp.arange(M)
        is_first = jnp.concatenate([jnp.ones((1,), bool), se[1:] != se[:-1]])
        group_starts = jax.lax.cummax(pos * is_first.astype(pos.dtype))
        slot = pos - group_starts
        valid = slot < C
        safe_slot = jnp.where(valid, slot, C)
        expert_in = jnp.zeros((E, C + 1, D), x.dtype).at[se, safe_slot].set(x_flat[st])
        expert_gate = jnp.zeros((E, C + 1), x.dtype).at[se, safe_slot].set(sg)
        expert_tok = jnp.full((E, C + 1), N, jnp.int32).at[se, safe_slot].set(st.astype(jnp.int32))
        expert_mask = jnp.zeros((E, C + 1), bool).at[se, safe_slot].set(valid)
        expert_in = expert_in[:, :C]
        expert_gate = expert_gate[:, :C]
        expert_tok = expert_tok[:, :C]
        expert_mask = expert_mask[:, :C]
        hg = jnp.einsum('ecd,efd->ecf', expert_in, w_gate)
        hu = jnp.einsum('ecd,efd->ecf', expert_in, w_up)
        expert_out = jnp.einsum('ecf,edf->ecd', jax.nn.silu(hg) * hu, w_down)
        fm = expert_mask.reshape(-1)
        dst = jnp.where(fm, expert_tok.reshape(-1), N)
        fg = jnp.where(fm, expert_gate.reshape(-1), jnp.zeros((), x.dtype))
        sparse = jax.ops.segment_sum(fg[:, None] * expert_out.reshape(-1, D), dst, num_segments=N + 1)[:N]
        return shared_out + sparse.reshape(B, S, D)
    h = _L0_tok_ref(x, L0_tok_fine_embed_w, L0_tok_coarse_embed_w, L0_tok_loc_to_cluster_w, L0_tok_loc_to_cluster_b)
    h = h + _L0_attn_ref(_layernorm(h, axis=-1), L0_attn_basis, L0_attn_q_coeffs, L0_attn_k_coeffs, L0_attn_v_coeffs, L0_attn_o_coeffs, L0_attn_decay_logit, L0_attn_mem_out_scale, L0_attn_read_coeffs, L0_attn_write_coeffs, L0_attn_channel_mix, L0_attn_bias, L0_attn_op_out_scale, L0_attn_mem_scale, L0_attn_op_scale)
    h = h + _L0_ffn_ref(_layernorm(h, axis=-1), L0_ffn_router_w, L0_ffn_bias, L0_ffn_shared_w_gate, L0_ffn_shared_w_up, L0_ffn_shared_w_down, L0_ffn_w_gate, L0_ffn_w_up, L0_ffn_w_down)
    return h

_drawn_inputs = setup_inputs


def setup_inputs(seed=0):
    import zlib

    import numpy as np

    out = dict(_drawn_inputs(seed))
    spreads = {'L0_attn_bias': (0.0, 2.0), 'L0_ffn_bias': (0.0, 2.0)}
    factors = {'L0_attn_read_coeffs': 64.0,
     'L0_attn_write_coeffs': 64.0,
     'L0_attn_channel_mix': 64.0,
     'L0_ffn_router_w': 64.0,
     'L0_ffn_shared_w_gate': 55.229,
     'L0_ffn_shared_w_up': 49.945,
     'L0_ffn_shared_w_down': 49.42,
     'L0_ffn_w_gate': 64.0,
     'L0_ffn_w_up': 64.0,
     'L0_ffn_w_down': 64.0}
    for name, (base, spread) in spreads.items():
        noise = np.random.default_rng([zlib.crc32(name.encode()), seed]).standard_normal(out[name].shape)
        drawn = base * np.exp(spread * noise) if base else spread * noise
        out[name] = jnp.asarray(drawn.astype(out[name].dtype))
    for name, factor in factors.items():
        out[name] = (out[name] * factor).astype(out[name].dtype)
    return out
```

```python
from contextlib import ExitStack

import concourse.bass as bass
from concourse import mybir

F32 = mybir.dt.float32
F32R = mybir.dt.float32r
I32 = mybir.dt.int32
ALU = mybir.AluOpType
ACT = mybir.ActivationFunctionType
AX = mybir.AxisListType

P = 128
BATCHES, SEQ = 8, 512
TILES = SEQ // P
HALF = 64
CLUSTERS = 64
D = 128
C = 128
EXPERTS, F, TOP = 64, 64, 6
SHARED = 2
CAPACITY = int(BATCHES * SEQ * TOP * 2.0 / EXPERTS)
ROUTED_PAIRS = EXPERTS // 2
PAIRS = ROUTED_PAIRS + SHARED // 2
RMS_EPS, LN_EPS, GATE_EPS = 1.1920929e-07, 1e-05, 1e-09
SENTINEL = 2.0
RING = 3
GATE_RING = 4
LAG = 3

AT_OUT = 4
AT_LOGITS = 0
AT_COARSE_IN = 5
AT_COARSE = 7
AT_XN = 10
AT_YZ = 12
AT_SCORES = 14
AT_MEM = 17
AT_XN2 = 20
AT_VALS = 21
AT_OP = 23
AT_X3 = 26
AT_ROUTER = 27
AT_GATES = 31

CHUNK = 11
CHUNKS = [(n, p0) for p0 in range(0, PAIRS, CHUNK) for n in ("gate", "up")] + \
    [("down", p0) for p0 in range(0, PAIRS, CHUNK)]
SPLIT_AT = [AT_LOGITS, AT_COARSE_IN, AT_COARSE, AT_XN, AT_YZ, AT_SCORES, AT_MEM, AT_XN2, AT_VALS]


def build(nc, ids, table, cluster_b, coarse_w, basis_t, q_c, k_c, v_c, o_c, read_t, write_t, mix, bias,
          decay_logit, mem_out_scale, op_out_scale, mem_scale, op_scale, router_t, router_b,
          gate_t, up_t, down_t, out):
    ctx = ExitStack()
    with ctx:
        def sb(name, shape, dt=F32):
            return ctx.enter_context(nc.sbuf_tensor(name, shape, dt))

        sems = {}

        def sem(name):
            if name not in sems:
                sems[name] = ctx.enter_context(nc.semaphore(name))
            return sems[name]

        idx = sb("idx", [P, BATCHES * TILES], I32)
        cluster_b_row = sb("cluster_b_row", [P, CLUSTERS])
        router_b_row = sb("router_b_row", [P, EXPERTS])
        coarse_sb = sb("coarse_sb", [CLUSTERS, HALF])
        basis = sb("basis", [P, D])
        small_w = {n: sb("w_" + n, [P, C]) for n in ("q", "k", "v", "o", "read", "write", "mix")}
        bias_col = sb("bias_col", [P, 1])
        scalars = sb("scalars", [P, 5])
        router_raw = sb("router_raw", [P, EXPERTS])
        router_hi = sb("router_hi", [P, EXPERTS], F32R)
        router_lo = sb("router_lo", [P, EXPERTS], F32R)

        w_hi = {n: sb(f"{n}_hi", [P, PAIRS, P], F32R) for n in ("gate", "up", "down")}
        w_lo = {n: sb(f"{n}_lo", [P, PAIRS, P], F32R) for n in ("gate", "up", "down")}

        ident = sb("ident", [P, P])
        steps = sb("steps", [P, P], I32)
        expo = sb("expo", [P, P])
        decay_full = sb("decay_full", [P, P])
        decay_mask = sb("decay_mask", [P, P])
        decay_out = sb("decay_out", [P, P])
        decay_cols = sb("decay_cols", [P, 3])
        decay_exps = sb("decay_exps", [P, 3])
        sig = sb("sig", [P, 1])
        mem_mul = sb("mem_mul", [P, 1])
        op_mul = sb("op_mul", [P, 1])
        neg_half = sb("neg_half", [P, TILES])
        ones_row = sb("ones_row", [EXPERTS, SEQ])
        qk_in = sb("qk_in", [P, P])
        vo_in = sb("vo_in", [P, P])
        qk_t = sb("qk_t", [P, P])
        vo_t = sb("vo_t", [P, P])
        qk_w = sb("qk_w", [P, P])
        vo_w = sb("vo_w", [P, P])
        read_e = sb("read_e", [P, P])
        read_s = sb("read_s", [P, P])
        read_stat = sb("read_stat", [P, 4])
        read_mix = sb("read_mix", [P, P])
        write_w = sb("write_w", [P, P])

        emb = [sb(f"emb{i}", [P, TILES, D]) for i in range(2)]
        lg = sb("lg", [P, TILES, CLUSTERS])
        lg2 = sb("lg2", [P, TILES, CLUSTERS])
        lge = sb("lge", [P, TILES, CLUSTERS])
        soft = sb("soft", [P, 3, TILES])
        lge_t = sb("lge_t", [CLUSTERS, SEQ])
        bn1 = sb("bn1", [P, TILES, 6])
        mv1 = sb("mv1", [P, TILES, 2])
        pool1 = sb("pool1", [P, 6, TILES])
        x1 = sb("x1", [P, TILES, D])
        xn = sb("xn", [P, TILES, D])
        xn_dec = sb("xn_dec", [P, TILES - 1, D])
        xn_t = sb("xn_t", [P, SEQ])
        y_t = sb("y_t", [P, SEQ])
        y_dec = sb("y_dec", [P, TILES - 1, P])
        z = sb("z", [P, TILES, D])
        scores = sb("scores", [P, TILES, P])
        state = sb("state", [P, TILES - 1, P])
        x2 = sb("x2", [P, TILES, D])
        x2_sq = sb("x2_sq", [P, D])
        ss2 = sb("ss2", [P, TILES])
        pool2 = sb("pool2", [P, 2, TILES])
        xn2, xn2_t, vals = xn, xn_t, y_t
        hx = sb("hx", [P, TILES, D])
        h2 = [sb(f"h2_{i}", [P, TILES, D]) for i in range(2)]
        bn3 = sb("bn3", [P, TILES, 6])
        mv3 = sb("mv3", [P, TILES, 2])
        pool3 = sb("pool3", [P, 2, TILES])
        x3 = xn
        x3_hi = [sb(f"x3_hi{i}", [P, SEQ], F32R) for i in range(2)]
        x3_lo = [sb(f"x3_lo{i}", [P, SEQ], F32R) for i in range(2)]
        rl = sb("rl", [P, TILES, EXPERTS])
        rl2 = sb("rl2", [P, TILES, EXPERTS])
        re = sb("re", [P, TILES, EXPERTS])
        rstat = sb("rstat", [P, 3, TILES])
        prob = sb("prob", [P, TILES, EXPERTS + 2])
        top8 = sb("top8", [P, TILES, 8])
        struck = sb("struck", [P, TILES, EXPERTS + 2])
        tstat = sb("tstat", [P, 3, TILES])
        chosen = sb("chosen", [P, TILES, EXPERTS])
        gate_n = sb("gate_n", [P, TILES, EXPERTS])
        gates = sb("gates", [P, TILES, EXPERTS])
        taken = sb("taken", [EXPERTS, SEQ])
        gates_t = sb("gates_t", [EXPERTS, SEQ])
        gate_rows = sb("gate_rows", [P, GATE_RING, SEQ])
        hid = sb("hid", [P, RING, SEQ])
        silu = gated = hid
        raw = [b.rearrange("p r s -> p (r s)")[:, 0:CHUNK * P].rearrange("p (c d) -> p c d", c=CHUNK)
               for b in (hid[:, :, :], gate_rows[:, :, :])]
        hid_hi = sb("hid_hi", [P, RING, SEQ], F32R)
        hid_lo = sb("hid_lo", [P, RING, SEQ], F32R)
        ffn_t = sb("ffn_t", [P, SEQ])
        result = sb("result", [P, TILES, D])
        gates_dram = nc.dram_tensor("gates_dram", (BATCHES, EXPERTS, SEQ), F32, kind="Internal").ap()

        def bank(name):
            return ctx.enter_context(nc.psum_tensor(name, [P, 512], F32))

        bank_g = [bank(f"bank_g{i}") for i in range(2)]
        bank_u = [bank(f"bank_u{i}") for i in range(2)]
        bank_y = [bank(f"bank_y{i}") for i in range(2)]
        bank_f = [bank(f"bank_f{i}") for i in range(2)]

        def tiles(b):
            return b[:, :].rearrange("p (t d) -> p t d", t=TILES)

        def over(col, n):
            return col.unsqueeze(2).to_broadcast([P, TILES, n])

        out_v = out.rearrange("b (t p) d -> b p t d", p=P)

        block = ctx.enter_context(nc.Block())

        def alone(eng, name):
            eng.sem_inc(sem(name), 1)

        def wait(eng, name, value):
            if isinstance(value, int) and value <= 0:
                return
            eng.wait_ge(sem(name), value)

        def gate_row_loads(sp, b, p):
            if p == 0:
                sp.wait_ge(sem("gates_stored"), 16 * b + 16)
                if isinstance(b, int) and b == 0:
                    sp.wait_ge(sem("split_lo"), len(CHUNKS))
            slot = p % GATE_RING
            wait(sp, "gated_done", PAIRS * b + (p - GATE_RING + 1 if p >= GATE_RING else p - GATE_RING))
            for e in range(2):
                src = gates_dram[b, 2 * p + e:2 * p + e + 1, :] if isinstance(b, int) else \
                    gates_dram[bass.ds(b, 1), 2 * p + e, :]
                sp.dma_start(gate_rows[F * e:F * e + F, slot, :],
                             src.to_broadcast([F, SEQ])).then_inc(sem(f"gate_rows{slot}"), 16)

        def sync_sequence(sp, b, par, front):
            for p in range(PAIRS):
                if p < ROUTED_PAIRS:
                    gate_row_loads(sp, b, p)
                if p == AT_OUT + 3 and not (isinstance(b, int) and b == 0):
                    store(sp, b - 1)
                if front and p == PAIRS - 1:
                    store_gates(sp, b + 1)

        def store_gates(sp, b):
            sp.wait_ge(sem("gates_t"), b + 1)
            dst = gates_dram[b] if isinstance(b, int) else \
                gates_dram[bass.ds(b, 1), :, :].rearrange("a e s -> (a e) s")
            sp.dma_start(dst, gates_t[:, :]).then_inc(sem("gates_stored"), 16)

        def store(sp, b):
            sp.wait_ge(sem("result"), b + 1)
            dst = out_v[b] if isinstance(b, int) else \
                out_v[bass.ds(b, 1), :, :, :].rearrange("a p t d -> (a p) t d")
            sp.dma_start(dst, result[:, :, :]).then_inc(sem("stored"), 16)

        @block.sync
        def _(sp):
            sp.dma_start(idx[:, :], ids).then_inc(sem("idx"), 16)
            sp.dma_start(cluster_b_row[:, :], cluster_b.to_broadcast([P, CLUSTERS])).then_inc(sem("cluster_b"), 16)
            sp.dma_start(basis[:, :], basis_t).then_inc(sem("small"), 16)
            for n, src in (("q", q_c), ("k", k_c), ("v", v_c), ("o", o_c)):
                sp.dma_start(small_w[n][:, :], src).then_inc(sem("small"), 16)
            for n, src in (("read", read_t), ("write", write_t), ("mix", mix)):
                sp.dma_start(small_w[n][:, :], src).then_inc(sem("small"), 16)
            sp.dma_start(coarse_sb[:, :], coarse_w).then_inc(sem("coarse_w"), 16)
            sp.dma_start(bias_col[:, :], bias).then_inc(sem("small"), 16)
            sp.dma_start(router_raw[:, :], router_t).then_inc(sem("router"), 16)
            sp.dma_start(router_b_row[:, :], router_b.to_broadcast([P, EXPERTS])).then_inc(sem("router"), 16)
            sources = {"gate": gate_t, "up": up_t, "down": down_t}
            for k, (n, p0) in enumerate(CHUNKS):
                if k >= 2:
                    sp.wait_ge(sem("split_lo"), k - 1)
                sp.dma_start(raw[k % 2][:, :, :], sources[n][:, p0:p0 + CHUNK, :]).then_inc(sem(f"raw{k % 2}"), 16)
            store_gates(sp, 0)
            sync_sequence(sp, 0, 0, True)
            with sp.Fori(0, (BATCHES - 2) // 2) as i:
                sync_sequence(sp, i * 2 + 1, 1, True)
                sync_sequence(sp, i * 2 + 2, 0, True)
            sync_sequence(sp, BATCHES - 1, 1, False)
            store(sp, BATCHES - 1)
            sp.wait_ge(sem("stored"), 16 * BATCHES + 16)
            sp.wait_ge(sem("gates_stored"), 16 * BATCHES)

        def pe_front(pe, b, par, p):
            f0, f1 = bank_f
            if p == AT_COARSE_IN:
                pe.wait_ge(sem("cluster_exp"), b + 1)
                alone(pe, "pe_passed")
                for t in range(TILES):
                    last = pe.transpose(f0[0:CLUSTERS, t * P:t * P + P], lge[:, t, :], ident[:, :])
                last.then_inc(sem("pe_exp_t"), 1)
            if p == AT_COARSE:
                pe.wait_ge(sem("exp_t"), b + 1)
                for t in range(TILES):
                    last = pe.matmul(f1[:, t * HALF:t * HALF + HALF], lge_t[:, t * P:t * P + P], coarse_sb[:, :],
                                     start=(t == 0), stop=(t == TILES - 1), skip_group_check=True)
                last.then_inc(sem("pe_coarse"), 1)
            if p == AT_XN:
                pe.wait_ge(sem("xn"), b + 1)
                for t in range(TILES):
                    last = pe.transpose(f0[:, t * P:t * P + P], xn[:, t, :], ident[:, :])
                last.then_inc(sem("pe_xn_t"), 1)
            if p == AT_YZ:
                pe.wait_ge(sem("xn_t"), b + 1)
                pe.matmul(f1[:, :], qk_w[:, :], xn_t[:, :], start=True, stop=True).then_inc(sem("pe_y"), 1)
                for t in range(TILES):
                    last = pe.matmul(f0[:, t * P:t * P + P], xn_t[:, t * P:t * P + P], vo_w[:, :],
                                     start=(t == 0), stop=(t == TILES - 1), skip_group_check=True)
                last.then_inc(sem("pe_z"), 1)
            if p == AT_SCORES:
                pe.wait_ge(sem("y_t"), b + 1)
                pe.wait_ge(sem("y_dec"), b + 1)
                for t in range(TILES):
                    last = pe.matmul(f1[:, t * P:t * P + P], xn_t[:, t * P:t * P + P], y_t[:, t * P:t * P + P],
                                     start=(t == 0), stop=(t == TILES - 1), skip_group_check=True)
                last.then_inc(sem("pe_scores"), 1)
                pe.wait_ge(sem("z"), b + 1)
                pe.wait_ge(sem("xn_dec"), b + 1)
                for t in range(1, TILES):
                    last = pe.matmul(f0[:, (t - 1) * P:t * P], xn_dec[:, t - 1, :], z[:, t, :],
                                     start=(t == 1), stop=(t == TILES - 1), skip_group_check=True)
                last.then_inc(sem("pe_state"), 1)
            if p == AT_MEM:
                pe.wait_ge(sem("scores"), b + 1)
                pe.wait_ge(sem("state"), b + 1)
                for t in range(TILES):
                    last = pe.matmul(f1[:, t * P:t * P + P], scores[:, t, :], z[:, t, :],
                                     start=(t == 0), stop=(t == TILES - 1), skip_group_check=True)
                    if t < TILES - 1:
                        last = pe.matmul(f1[:, t * P:t * P + P], y_dec[:, t, :], state[:, t, :],
                                         start=False, stop=False, skip_group_check=True)
                last.then_inc(sem("pe_mem"), 1)
            if p == AT_XN2:
                pe.wait_ge(sem("xn2"), b + 1)
                for t in range(TILES):
                    last = pe.transpose(f0[:, t * P:t * P + P], xn2[:, t, :], ident[:, :])
                last.then_inc(sem("pe_xn2_t"), 1)
            if p == AT_VALS:
                pe.wait_ge(sem("xn2_t"), b + 1)
                pe.matmul(f1[:, :], read_mix[:, :], xn2_t[:, :], start=True, stop=True).then_inc(sem("pe_vals"), 1)
            if p == AT_OP:
                pe.wait_ge(sem("vals"), b + 1)
                for t in range(TILES):
                    last = pe.matmul(f0[:, t * P:t * P + P], vals[:, t * P:t * P + P], write_w[:, :],
                                     start=(t == 0), stop=(t == TILES - 1), skip_group_check=True)
                last.then_inc(sem("pe_op"), 1)
            if p == AT_X3:
                pe.wait_ge(sem("x3"), b + 1)
                for t in range(TILES):
                    last = pe.transpose(f1[:, t * P:t * P + P], x3[:, t, :], ident[:, :])
                last.then_inc(sem("pe_x3_t"), 1)
            if p == AT_ROUTER:
                pe.wait_ge(sem("x3_hi"), b + 1)
                pe.wait_ge(sem("x3_lo"), b + 1)
                for t in range(TILES):
                    c = slice(t * P, t * P + P)
                    o = f0[:, t * EXPERTS:(t + 1) * EXPERTS]
                    pe.matmul(o, x3_hi[par][:, c], router_hi[:, :], start=(t == 0), stop=False, skip_group_check=True)
                    pe.matmul(o, x3_lo[par][:, c], router_hi[:, :], start=False, stop=False, skip_group_check=True)
                    last = pe.matmul(o, x3_hi[par][:, c], router_lo[:, :], start=False, stop=(t == TILES - 1),
                                     skip_group_check=True)
                last.then_inc(sem("pe_router"), 1)
            if p == AT_GATES:
                pe.wait_ge(sem("chosen"), b + 1)
                alone(pe, "pe_passed")
                for t in range(TILES):
                    last = pe.transpose(f1[0:EXPERTS, t * P:t * P + P], chosen[:, t, :], ident[:, :])
                last.then_inc(sem("pe_chosen_t"), 1)
                pe.wait_ge(sem("gates"), b + 1)
                alone(pe, "pe_passed")
                for t in range(TILES):
                    last = pe.transpose(f0[0:EXPERTS, t * P:t * P + P], gates[:, t, :], ident[:, :])
                last.then_inc(sem("pe_gates_t"), 1)

        def down(pe, b, par, p):
            q = PAIRS * b + p
            if isinstance(b, int) and b == 0 and p == 0:
                pe.wait_ge(sem("split_hi"), len(CHUNKS))
                pe.wait_ge(sem("split_lo"), len(CHUNKS))
            pe.wait_ge(sem("hid_hi"), q + 1)
            pe.wait_ge(sem("hid_lo"), q + 1)
            s, y = p % RING, bank_y[par]
            pe.matmul(y[:, :], w_hi["down"][:, p, :], hid_hi[:, s, :], start=(p == 0), stop=False)
            pe.matmul(y[:, :], w_lo["down"][:, p, :], hid_hi[:, s, :], start=False, stop=False)
            pe.matmul(y[:, :], w_hi["down"][:, p, :], hid_lo[:, s, :], start=False,
                      stop=(p == PAIRS - 1)).then_inc(sem("down_done"), 1)

        def pe_out(pe, b):
            pe.wait_ge(sem("ffn_t"), b + 1)
            for t in range(TILES):
                last = pe.transpose(bank_f[1][:, t * P:t * P + P], ffn_t[:, t * P:t * P + P], ident[:, :])
            last.then_inc(sem("pe_out"), 1)

        def pe_sequence(pe, b, par, front):
            first = isinstance(b, int) and b == 0
            for p in range(PAIRS):
                q = PAIRS * b + p
                ring = (p + par) % 2
                for name, banks, freed in (("gate", bank_g, "silu_done"), ("up", bank_u, "hid")):
                    wait(pe, freed, q - 1)
                    o = banks[ring][:, :]
                    pe.matmul(o, w_hi[name][:, p, :], x3_hi[par][:, :], start=True, stop=False)
                    pe.matmul(o, w_lo[name][:, p, :], x3_hi[par][:, :], start=False, stop=False)
                    pe.matmul(o, w_hi[name][:, p, :], x3_lo[par][:, :], start=False,
                              stop=True).then_inc(sem("pe_" + name), 1)
                if p >= LAG:
                    down(pe, b, par, p - LAG)
                elif not first:
                    down(pe, b - 1, 1 - par, p - LAG + PAIRS)
                if p == AT_OUT and not first:
                    pe_out(pe, b - 1)
                if front:
                    pe_front(pe, b + 1, 1 - par, p)

        @block.tensor
        def _(pe):
            f0, f1 = bank_f
            pe.wait_ge(sem("small"), 16 * 9)
            pe.wait_ge(sem("ident"), 2)
            pe.matmul(f0[:, 0:P], small_w["q"][:, :], small_w["k"][:, :], start=True, stop=True)
            pe.matmul(f0[:, P:2 * P], small_w["v"][:, :], small_w["o"][:, :], start=True, stop=True,
                      skip_group_check=True)
            pe.matmul(f0[:, 2 * P:3 * P], small_w["read"][:, :], basis[:, :], start=True, stop=True,
                      skip_group_check=True)
            pe.matmul(f0[:, 3 * P:4 * P], small_w["write"][:, :], basis[:, :], start=True, stop=True,
                      skip_group_check=True).then_inc(sem("pe_prep"), 1)
            pe.wait_ge(sem("prep1"), 1)
            pe.matmul(f1[:, 0:P], qk_in[:, :], basis[:, :], start=True, stop=True)
            pe.matmul(f1[:, P:2 * P], vo_in[:, :], basis[:, :], start=True, stop=True,
                      skip_group_check=True).then_inc(sem("pe_prep"), 1)
            pe.wait_ge(sem("prep2"), 1)
            pe.matmul(f0[:, 0:P], qk_t[:, :], basis[:, :], start=True, stop=True, skip_group_check=True)
            pe.matmul(f0[:, P:2 * P], vo_t[:, :], basis[:, :], start=True, stop=True, skip_group_check=True)
            pe.matmul(f0[:, 2 * P:3 * P], read_s[:, :], small_w["mix"][:, :], start=True, stop=True,
                      skip_group_check=True).then_inc(sem("pe_prep"), 1)
            pe.wait_ge(sem("prep3"), 1)
            pe.wait_ge(sem("coarse_w"), 16)
            for p in range(PAIRS):
                pe_front(pe, 0, 0, p)
                if p == AT_ROUTER - 1:
                    pe.wait_ge(sem("router_split"), 2)
            pe.wait_ge(sem("split_lo"), 2 * PAIRS // CHUNK)
            pe.wait_ge(sem("split_hi"), 2 * PAIRS // CHUNK)
            pe_sequence(pe, 0, 0, True)
            with pe.Fori(0, (BATCHES - 2) // 2) as i:
                pe_sequence(pe, i * 2 + 1, 1, True)
                pe_sequence(pe, i * 2 + 2, 0, True)
            last = BATCHES - 1
            pe_sequence(pe, last, 1, False)
            for p in range(PAIRS - LAG, PAIRS):
                down(pe, last, 1, p)
            pe_out(pe, last)

        def act_front(act, b, par, p):
            f0, f1 = bank_f
            if p == AT_LOGITS:
                act.wait_ge(sem("cluster_logits"), b + 1)
                act.activation(lge[:, :, :], lg2[:, :, :], ACT.Exp).then_inc(sem("cluster_exp"), 1)
            if p == AT_COARSE_IN:
                act.wait_ge(sem("pe_exp_t"), b + 1)
                act.activation(lge_t[:, :], f0[0:CLUSTERS, :], ACT.Copy).then_inc(sem("exp_t"), 1)
            if p == AT_XN:
                act.wait_ge(sem("pe_xn_t"), b + 1)
                act.activation(xn_t[:, :], f0[:, :], ACT.Copy).then_inc(sem("xn_t"), 1)
            if p == AT_YZ:
                act.wait_ge(sem("pe_y"), b + 1)
                act.activation(y_t[:, :], f1[:, :], ACT.Copy).then_inc(sem("y_t"), 1)
                act.wait_ge(sem("pe_z"), b + 1)
                act.activation(z[:, :, :], tiles(f0), ACT.Copy).then_inc(sem("z"), 1)
            if p == AT_MEM + 1:
                act.wait_ge(sem("x2"), b + 1)
                for t in range(TILES):
                    if t:
                        act.wait_ge(sem("x2_squares"), TILES * b + t)
                    act.activation(x2_sq[:, :], x2[:, t, :], ACT.Square,
                                   accum_out=ss2[:, t:t + 1]).then_inc(sem("x2_squares"), 1)
            if p == AT_XN2:
                act.wait_ge(sem("pe_xn2_t"), b + 1)
                act.activation(xn2_t[:, :], f0[:, :], ACT.Copy).then_inc(sem("xn2_t"), 1)
            if p == AT_VALS:
                act.wait_ge(sem("pe_vals"), b + 1)
                act.activation(vals[:, :], f1[:, :], ACT.Gelu, bias=bias_col[:, 0:1]).then_inc(sem("vals"), 1)
            if p == AT_X3:
                act.wait_ge(sem("pe_x3_t"), b + 1)
                act.activation(x3_hi[par][:, :], f1[:, :], ACT.Copy).then_inc(sem("x3_hi"), 1)
            if p == AT_ROUTER:
                act.wait_ge(sem("router_logits"), b + 1)
                act.activation(re[:, :, :], rl2[:, :, :], ACT.Exp).then_inc(sem("router_exp"), 1)

        def act_silu(act, b, par, p):
            q = PAIRS * b + p
            act.wait_ge(sem("pe_gate"), q + 1)
            wait(act, "hid_lo", q - RING + 1)
            if isinstance(b, int) and b == 0 and p == 0:
                act.wait_ge(sem("split_lo"), len(CHUNKS))
            act.activation(silu[:, p % RING, :], bank_g[(p + par) % 2][:, :], ACT.Silu).then_inc(sem("silu_done"), 1)

        def act_hi(act, b, p):
            q = PAIRS * b + p
            act.wait_ge(sem("hid"), q + 1)
            wait(act, "down_done", q - RING + 1)
            act.activation(hid_hi[:, p % RING, :], hid[:, p % RING, :], ACT.Copy).then_inc(sem("hid_hi"), 1)

        def act_copy_out(act, b, par):
            act.wait_ge(sem("down_done"), PAIRS * b + PAIRS)
            act.activation(ffn_t[:, :], bank_y[par][:, :], ACT.Copy).then_inc(sem("ffn_t"), 1)

        def act_sequence(act, b, par, front):
            first = isinstance(b, int) and b == 0
            for p in range(PAIRS):
                act_silu(act, b, par, p)
                if p:
                    act_hi(act, b, p - 1)
                elif not first:
                    act_hi(act, b - 1, PAIRS - 1)
                if p == LAG and not first:
                    act_copy_out(act, b - 1, 1 - par)
                if front:
                    act_front(act, b + 1, 1 - par, p)

        @block.scalar
        def _(act):
            act.wait_ge(sem("scalars"), 16 * 5)
            act.activation(sig[:, :], scalars[:, 0:1], ACT.Sigmoid).then_inc(sem("sigmoid"), 1)
            act.wait_ge(sem("read_shifted"), 1)
            act.activation(read_e[:, :], read_s[:, :], ACT.Exp, accum_out=read_stat[:, 1:2])\
               .then_inc(sem("read_exp"), 1)
            act.wait_ge(sem("router"), 32)
            act.activation(router_hi[:, :], router_raw[:, :], ACT.Copy).then_inc(sem("router_split"), 1)
            for p in range(PAIRS):
                act_front(act, 0, 0, p)
                if p in SPLIT_AT:
                    k = SPLIT_AT.index(p)
                    n, p0 = CHUNKS[k]
                    act.wait_ge(sem(f"raw{k % 2}"), 16 * (k // 2 + 1))
                    act.activation(w_hi[n][:, p0:p0 + CHUNK, :], raw[k % 2][:, :, :], ACT.Copy)\
                       .then_inc(sem("split_hi"), 1)
            act_sequence(act, 0, 0, True)
            with act.Fori(0, (BATCHES - 2) // 2) as i:
                act_sequence(act, i * 2 + 1, 1, True)
                act_sequence(act, i * 2 + 2, 0, True)
            last = BATCHES - 1
            act_sequence(act, last, 1, False)
            act_hi(act, last, PAIRS - 1)
            act_copy_out(act, last, 1)

        def dve_front(dve, b, par, p, slot_use):
            f0, f1 = bank_f

            if p == AT_LOGITS:
                e = emb[par]
                dve.wait_ge(sem(f"gathered{par}"), 16 * TILES * slot_use)
                dve.tensor_tensor(lg[:, :, :], e[:, :, HALF:D],
                                  cluster_b_row[:, :].unsqueeze(1).to_broadcast([P, TILES, CLUSTERS]),
                                  ALU.add).then_inc(sem("lg"), 1)
                dve.wait_ge(sem("lg"), b + 1)
                dve.tensor_reduce(soft[:, 0, :], lg[:, :, :], AX.X, ALU.max).then_inc(sem("lg_max"), 1)
                dve.wait_ge(sem("lg_max"), b + 1)
                dve.tensor_tensor(lg2[:, :, :], lg[:, :, :], over(soft[:, 0, :], CLUSTERS), ALU.subtract)\
                   .then_inc(sem("cluster_logits"), 1)
                dve.wait_ge(sem("cluster_exp"), b + 1)
                dve.tensor_reduce(soft[:, 1, :], lge[:, :, :], AX.X, ALU.add).then_inc(sem("lg_sum"), 1)
                dve.wait_ge(sem("lg_sum"), b + 1)
                dve.reciprocal(soft[:, 2, :], soft[:, 1, :]).then_inc(sem("lg_inv"), 1)
            if p == AT_COARSE:
                e = emb[par]
                dve.wait_ge(sem("pe_coarse"), b + 1)
                dve.wait_ge(sem("lg_inv"), b + 1)
                dve.tensor_tensor(e[:, :, HALF:D], f1[:, 0:TILES * HALF].rearrange("p (t d) -> p t d", t=TILES),
                                  over(soft[:, 2, :], HALF), ALU.mult).then_inc(sem("h"), 1)
                dve.wait_ge(sem("h"), b + 1)
                for t in range(TILES):
                    dve.bn_stats(bn1[:, t, :], e[:, t, :]).then_inc(sem("bn1"), 1)
                dve.wait_ge(sem("bn1"), TILES * b + TILES)
                alone(dve, "dve_passed")
                for t in range(TILES):
                    last = dve.bn_aggr(mv1[:, t, :], bn1[:, t, :])
                last.then_inc(sem("mv1"), 1)
                dve.wait_ge(sem("x1_inv"), b + 1)
                for t in range(TILES):
                    last = dve.tensor_scalar(x1[:, t, :], e[:, t, :], mv1[:, t, 0:1], pool1[:, 1, t:t + 1],
                                             ALU.subtract, ALU.mult)
                last.then_inc(sem("x1"), 1)
                dve.wait_ge(sem("xn_inv"), b + 1)
                dve.wait_ge(sem("x1"), b + 1)
                for t in range(TILES):
                    last = dve.tensor_scalar(xn[:, t, :], x1[:, t, :], pool1[:, 5, t:t + 1], None, ALU.mult)
                last.then_inc(sem("xn"), 1)
                dve.wait_ge(sem("xn"), b + 1)
                dve.tensor_scalar(xn_dec[:, :, :], xn[:, 1:TILES, :], decay_cols[:, 0:1], None, ALU.mult)\
                   .then_inc(sem("xn_dec"), 1)
            if p == AT_YZ:
                dve.wait_ge(sem("y_t"), b + 1)
                dve.tensor_tensor(y_dec[:, :, :], y_t[:, 0:(TILES - 1) * P].rearrange("p (t d) -> p t d", d=P),
                                  decay_out[:, :].unsqueeze(1).to_broadcast([P, TILES - 1, P]), ALU.mult)\
                   .then_inc(sem("y_dec"), 1)
            if p == AT_SCORES:
                dve.wait_ge(sem("pe_scores"), b + 1)
                dve.tensor_tensor(scores[:, :, :], tiles(f1),
                                  decay_mask[:, :].unsqueeze(1).to_broadcast([P, TILES, P]), ALU.mult)\
                   .then_inc(sem("scores"), 1)
                dve.wait_ge(sem("pe_state"), b + 1)
                dve.tensor_copy(state[:, TILES - 2, :], f0[:, (TILES - 2) * P:(TILES - 1) * P])\
                   .then_inc(sem("state_part"), 1)
                for k, c in enumerate(range(TILES - 3, -1, -1)):
                    dve.wait_ge(sem("state_part"), (TILES - 2) * b + k + 1)
                    dve.scalar_tensor_tensor(state[:, c, :], state[:, c + 1, :], decay_cols[:, 1:2],
                                             f0[:, c * P:c * P + P], ALU.mult, ALU.add)\
                       .then_inc(sem("state_part" if c else "state"), 1)
            if p == AT_MEM:
                dve.wait_ge(sem("pe_mem"), b + 1)
                dve.scalar_tensor_tensor(x2[:, :, :], tiles(f1), mem_mul[:, 0:1], x1[:, :, :], ALU.mult, ALU.add)\
                   .then_inc(sem("x2"), 1)
            if p == AT_MEM + 1:
                dve.wait_ge(sem("xn2_inv"), b + 1)
                for t in range(TILES):
                    last = dve.tensor_scalar(xn2[:, t, :], x2[:, t, :], pool2[:, 1, t:t + 1], None, ALU.mult)
                last.then_inc(sem("xn2"), 1)
            if p == AT_OP:
                dve.wait_ge(sem("pe_op"), b + 1)
                dve.wait_ge(sem("hx"), b + 1)
                dve.scalar_tensor_tensor(h2[par][:, :, :], tiles(f0), op_mul[:, 0:1], hx[:, :, :], ALU.mult, ALU.add)\
                   .then_inc(sem("h2"), 1)
                dve.wait_ge(sem("h2"), b + 1)
                for t in range(TILES):
                    dve.bn_stats(bn3[:, t, :], h2[par][:, t, :]).then_inc(sem("bn3"), 1)
                dve.wait_ge(sem("bn3"), TILES * b + TILES)
                alone(dve, "dve_passed")
                for t in range(TILES):
                    last = dve.bn_aggr(mv3[:, t, :], bn3[:, t, :])
                last.then_inc(sem("mv3"), 1)
                dve.wait_ge(sem("x3_inv"), b + 1)
                for t in range(TILES):
                    last = dve.tensor_scalar(x3[:, t, :], h2[par][:, t, :], mv3[:, t, 0:1], pool3[:, 1, t:t + 1],
                                             ALU.subtract, ALU.mult)
                last.then_inc(sem("x3"), 1)
            if p == AT_X3:
                dve.wait_ge(sem("x3_hi"), b + 1)
                dve.tensor_tensor(x3_lo[par][:, :], f1[:, :], x3_hi[par][:, :].bitcast(F32), ALU.subtract)\
                   .then_inc(sem("x3_lo"), 1)
            if p == AT_ROUTER:
                dve.wait_ge(sem("pe_router"), b + 1)
                dve.tensor_tensor(rl[:, :, :], f0[:, 0:TILES * EXPERTS].rearrange("p (t e) -> p t e", t=TILES),
                                  router_b_row[:, :].unsqueeze(1).to_broadcast([P, TILES, EXPERTS]), ALU.add)\
                   .then_inc(sem("rl"), 1)
                dve.wait_ge(sem("rl"), b + 1)
                dve.tensor_reduce(rstat[:, 0, :], rl[:, :, :], AX.X, ALU.max).then_inc(sem("rl_max"), 1)
                dve.wait_ge(sem("rl_max"), b + 1)
                dve.tensor_tensor(rl2[:, :, :], rl[:, :, :], over(rstat[:, 0, :], EXPERTS), ALU.subtract)\
                   .then_inc(sem("router_logits"), 1)
            if p == AT_ROUTER + 1:
                dve.wait_ge(sem("router_exp"), b + 1)
                dve.tensor_reduce(rstat[:, 1, :], re[:, :, :], AX.X, ALU.add).then_inc(sem("re_sum"), 1)
                dve.wait_ge(sem("re_sum"), b + 1)
                dve.reciprocal(rstat[:, 2, :], rstat[:, 1, :]).then_inc(sem("re_inv"), 1)
                dve.wait_ge(sem("re_inv"), b + 1)
                dve.tensor_tensor(prob[:, :, 2:], re[:, :, :], over(rstat[:, 2, :], EXPERTS), ALU.mult)\
                   .then_inc(sem("prob"), 1)
                dve.wait_ge(sem("prob"), b + 1)
                alone(dve, "dve_passed")
                for t in range(TILES):
                    dve.max(top8[:, t, :], prob[:, t, :]).then_inc(sem("top8"), 1)
                dve.wait_ge(sem("top8"), TILES * b + TILES)
                alone(dve, "dve_passed")
                for t in range(TILES):
                    last = dve.match_replace(struck[:, t, :], top8[:, t, :], prob[:, t, :], -1.0)
                last.then_inc(sem("struck"), 1)
                dve.tensor_reduce(tstat[:, 0, :], top8[:, :, 2:], AX.X, ALU.add).then_inc(sem("top_sum"), 1)
                dve.wait_ge(sem("struck"), b + 1)
                dve.tensor_scalar(chosen[:, :, :], struck[:, :, 2:], 0.0, None, ALU.is_lt).then_inc(sem("chosen"), 1)
                dve.wait_ge(sem("top_sum"), b + 1)
                dve.tensor_scalar(tstat[:, 1, :], tstat[:, 0, :], GATE_EPS, None, ALU.add).then_inc(sem("top_eps"), 1)
                dve.wait_ge(sem("top_eps"), b + 1)
                dve.reciprocal(tstat[:, 2, :], tstat[:, 1, :]).then_inc(sem("top_inv"), 1)
                dve.wait_ge(sem("top_inv"), b + 1)
                dve.tensor_tensor(gate_n[:, :, :], prob[:, :, 2:], over(tstat[:, 2, :], EXPERTS), ALU.mult)\
                   .then_inc(sem("gate_n"), 1)
                dve.wait_ge(sem("gate_n"), b + 1)
                dve.wait_ge(sem("chosen"), b + 1)
                dve.tensor_tensor(gates[:, :, :], gate_n[:, :, :], chosen[:, :, :], ALU.mult).then_inc(sem("gates"), 1)
            if p == AT_GATES:
                dve.wait_ge(sem("pe_chosen_t"), b + 1)
                wait(dve, "taken", b)
                first = isinstance(b, int) and b == 0
                if not first:
                    dve.tensor_copy(taken_end[:, :], taken[:, SEQ - 1:SEQ]).then_inc(sem("taken_end"), 1)
                    dve.wait_ge(sem("taken_end"), b)
                dve.tensor_tensor_scan(taken[:, :], ones_row[:, :], f1[0:EXPERTS, :],
                                       0.0 if first else taken_end[:, :], ALU.mult, ALU.add)\
                   .then_inc(sem("taken"), 1)
                dve.wait_ge(sem("taken"), b + 1)
                dve.wait_ge(sem("pe_gates_t"), b + 1)
                wait(dve, "gates_stored", 16 * b)
                dve.scalar_tensor_tensor(gates_t[:, :], taken[:, :], float(CAPACITY), f0[0:EXPERTS, :],
                                         ALU.is_le, ALU.mult).then_inc(sem("gates_t"), 1)

        taken_end = sb("taken_end", [EXPERTS, 1])

        def dve_hid(dve, b, par, p):
            q = PAIRS * b + p
            dve.wait_ge(sem("gated_done"), q + 1)
            dve.wait_ge(sem("pe_up"), q + 1)
            dve.tensor_tensor(hid[:, p % RING, :], gated[:, p % RING, :], bank_u[(p + par) % 2][:, :], ALU.mult)\
               .then_inc(sem("hid"), 1)

        def dve_lo(dve, b, p):
            q = PAIRS * b + p
            dve.wait_ge(sem("hid_hi"), q + 1)
            s = p % RING
            dve.tensor_tensor(hid_lo[:, s, :], hid[:, s, :], hid_hi[:, s, :].bitcast(F32), ALU.subtract)\
               .then_inc(sem("hid_lo"), 1)

        def dve_out(dve, b, par):
            dve.wait_ge(sem("pe_out"), b + 1)
            dve.wait_ge(sem("stored"), 16 * b + 16)
            dve.tensor_tensor(result[:, :, :], tiles(bank_f[1]), h2[par][:, :, :], ALU.add).then_inc(sem("result"), 1)

        def dve_sequence(dve, b, par, front, slot_use=0):
            first = isinstance(b, int) and b == 0
            for p in range(PAIRS):
                dve_hid(dve, b, par, p)
                if p:
                    dve_lo(dve, b, p - 1)
                elif not first:
                    dve_lo(dve, b - 1, PAIRS - 1)
                if p == AT_OUT and not first:
                    dve_out(dve, b - 1, 1 - par)
                if front:
                    dve_front(dve, b + 1, 1 - par, p, slot_use)

        @block.vector
        def _(dve):
            dve.sem_inc(sem("stored"), 16)
            dve.memset(ones_row[:, :], 1.0).then_inc(sem("ones"), 1)
            dve.memset(prob[:, :, 0:2], SENTINEL).then_inc(sem("sentinel"), 1)
            dve.wait_ge(sem("scalars"), 16 * 5)
            dve.tensor_tensor(mem_mul[:, :], scalars[:, 1:2], scalars[:, 3:4], ALU.mult).then_inc(sem("muls"), 1)
            dve.tensor_tensor(op_mul[:, :], scalars[:, 2:3], scalars[:, 4:5], ALU.mult).then_inc(sem("muls"), 1)
            dve.wait_ge(sem("cluster_b"), 16)
            dve.wait_ge(sem("pe_prep"), 1)
            dve.tensor_reduce(read_stat[:, 0:1], bank_f[0][:, 2 * P:3 * P], AX.X, ALU.max).then_inc(sem("read_max"), 1)
            dve.tensor_copy(qk_in[:, :], bank_f[0][:, 0:P])
            dve.tensor_copy(vo_in[:, :], bank_f[0][:, P:2 * P])
            dve.tensor_copy(write_w[:, :], bank_f[0][:, 3 * P:4 * P]).then_inc(sem("prep1"), 1)
            dve.wait_ge(sem("read_max"), 1)
            dve.tensor_scalar(read_s[:, :], bank_f[0][:, 2 * P:3 * P], read_stat[:, 0:1], None, ALU.subtract)\
               .then_inc(sem("read_shifted"), 1)
            dve.wait_ge(sem("pe_prep"), 2)
            dve.tensor_copy(qk_t[:, :], bank_f[1][:, 0:P])
            dve.tensor_copy(vo_t[:, :], bank_f[1][:, P:2 * P])
            dve.wait_ge(sem("read_exp"), 1)
            dve.reciprocal(read_stat[:, 2:3], read_stat[:, 1:2]).then_inc(sem("read_inv"), 1)
            dve.wait_ge(sem("read_inv"), 1)
            dve.tensor_scalar(read_s[:, :], read_e[:, :], read_stat[:, 2:3], None, ALU.mult).then_inc(sem("prep2"), 1)
            dve.wait_ge(sem("pe_prep"), 3)
            dve.tensor_copy(qk_w[:, :], bank_f[0][:, 0:P])
            dve.tensor_copy(vo_w[:, :], bank_f[0][:, P:2 * P])
            dve.tensor_copy(read_mix[:, :], bank_f[0][:, 2 * P:3 * P]).then_inc(sem("prep3"), 1)
            dve.wait_ge(sem("sentinel"), 1)
            dve.wait_ge(sem("ones"), 1)
            dve.wait_ge(sem("muls"), 2)
            dve.wait_ge(sem("router_split"), 1)
            dve.tensor_tensor(router_lo[:, :], router_raw[:, :], router_hi[:, :].bitcast(F32), ALU.subtract)\
               .then_inc(sem("router_split"), 1)
            for p in range(PAIRS):
                if p == AT_COARSE:
                    dve.wait_ge(sem("decays"), 3)
                dve_front(dve, 0, 0, p, 1)
                if p in SPLIT_AT:
                    k = SPLIT_AT.index(p)
                    n, p0 = CHUNKS[k]
                    dve.wait_ge(sem("split_hi"), k + 1)
                    dve.tensor_tensor(w_lo[n][:, p0:p0 + CHUNK, :], raw[k % 2][:, :, :],
                                      w_hi[n][:, p0:p0 + CHUNK, :].bitcast(F32), ALU.subtract)\
                       .then_inc(sem("split_lo"), 1)
            dve_sequence(dve, 0, 0, True, 1)
            with dve.Fori(0, (BATCHES - 2) // 2) as i:
                dve_sequence(dve, i * 2 + 1, 1, True, i + 2)
                dve_sequence(dve, i * 2 + 2, 0, True, i + 2)
            last = BATCHES - 1
            dve_sequence(dve, last, 1, False)
            dve_lo(dve, last, PAIRS - 1)
            dve_out(dve, last, 1)

        def gather(pool, b, par):
            wait(pool, "hx", b - 1)
            if not isinstance(b, int):
                pool.wait_ge(sem(f"gathered{1 - par}"), (b - 2 + par) * (8 * TILES) + 16 * TILES)
                pool.tensor_copy(idx_now[:, :], idx[:, bass.ds(b * TILES, TILES)]).then_inc(sem("idx_now"), 1)
                pool.wait_ge(sem("idx_now"), b - 2)
                alone(pool, "pool_passed")
            for t in range(TILES):
                at = idx[:, b * TILES + t:b * TILES + t + 1] if isinstance(b, int) else idx_now[:, t:t + 1]
                pool.indirect_dma_start(emb[par][:, t, :], None, table[:, :],
                                        bass.IndirectOffsetOnAxis(ap=at, axis=0))\
                    .then_inc(sem(f"gathered{par}"), 16)

        idx_now = sb("idx_now", [P, TILES], I32)

        def pool_front(pool, b, par, p):
            if p == AT_COARSE:
                pool.wait_ge(sem("mv1"), b + 1)
                alone(pool, "pool_passed")
                pool.tensor_scalar(pool1[:, 0, :], mv1[:, :, 1], LN_EPS, None, ALU.add).then_inc(sem("p1"), 1)
                pool.wait_ge(sem("p1"), 4 * b + 1)
                pool.tensor_tensor(pool1[:, 1, :], pool1[:, 0, :], neg_half[:, :], ALU.pow).then_inc(sem("x1_inv"), 1)
                pool.wait_ge(sem("x1_inv"), b + 1)
                pool.tensor_tensor(pool1[:, 2, :], pool1[:, 1, :], pool1[:, 1, :], ALU.mult).then_inc(sem("p1"), 1)
                pool.wait_ge(sem("p1"), 4 * b + 2)
                pool.tensor_tensor(pool1[:, 3, :], pool1[:, 2, :], mv1[:, :, 1], ALU.mult).then_inc(sem("p1"), 1)
                pool.wait_ge(sem("p1"), 4 * b + 3)
                alone(pool, "pool_passed")
                pool.tensor_scalar(pool1[:, 4, :], pool1[:, 3, :], RMS_EPS, None, ALU.add).then_inc(sem("p1"), 1)
                pool.wait_ge(sem("p1"), 4 * b + 4)
                pool.tensor_tensor(pool1[:, 5, :], pool1[:, 4, :], neg_half[:, :], ALU.pow).then_inc(sem("xn_inv"), 1)
            if p == AT_MEM + 1:
                pool.wait_ge(sem("x2_squares"), TILES * b + TILES)
                alone(pool, "pool_passed")
                pool.tensor_scalar(pool2[:, 0, :], ss2[:, :], 1.0 / D, RMS_EPS, ALU.mult, ALU.add).then_inc(sem("p2"), 1)
                pool.wait_ge(sem("p2"), b + 1)
                pool.tensor_tensor(pool2[:, 1, :], pool2[:, 0, :], neg_half[:, :], ALU.pow).then_inc(sem("xn2_inv"), 1)
                pool.wait_ge(sem("h"), b + 1)
                pool.tensor_tensor(hx[:, :, :], emb[par][:, :, :], x2[:, :, :], ALU.add).then_inc(sem("hx"), 1)
            if p == AT_OP:
                pool.wait_ge(sem("mv3"), b + 1)
                alone(pool, "pool_passed")
                pool.tensor_scalar(pool3[:, 0, :], mv3[:, :, 1], LN_EPS, None, ALU.add).then_inc(sem("p3"), 1)
                pool.wait_ge(sem("p3"), b + 1)
                pool.tensor_tensor(pool3[:, 1, :], pool3[:, 0, :], neg_half[:, :], ALU.pow).then_inc(sem("x3_inv"), 1)

        def pool_sequence(pool, b, par, front):
            for p in range(PAIRS):
                q = PAIRS * b + p
                pool.wait_ge(sem("silu_done"), q + 1)
                if p >= ROUTED_PAIRS:
                    alone(pool, "pool_passed")
                if p < ROUTED_PAIRS:
                    slot = p % GATE_RING
                    uses = ROUTED_PAIRS // GATE_RING
                    pool.wait_ge(sem(f"gate_rows{slot}"), 32 * uses * b + 32 * (p // GATE_RING + 1))
                    pool.tensor_tensor(gated[:, p % RING, :], silu[:, p % RING, :], gate_rows[:, slot, :], ALU.mult)\
                        .then_inc(sem("gated_done"), 1)
                else:
                    pool.tensor_scalar(gated[:, p % RING, :], silu[:, p % RING, :], 1.0 / SHARED, None, ALU.mult)\
                        .then_inc(sem("gated_done"), 1)
                if front:
                    pool_front(pool, b + 1, 1 - par, p)
                    if p == AT_OP + 1 and not (isinstance(b, int) and b + 2 >= BATCHES):
                        gather(pool, b + 2, par)

        @block.gpsimd
        def _(pool):
            for k, src in enumerate((decay_logit, mem_out_scale, op_out_scale, mem_scale, op_scale)):
                pool.dma_start(scalars[:, k:k + 1], src.to_broadcast([P, 1])).then_inc(sem("scalars"), 16)
            pool.wait_ge(sem("idx"), 16)
            gather(pool, 0, 0)
            pool.memset(ident[:, :], 0.0).then_inc(sem("ident"), 1)
            pool.wait_ge(sem("ident"), 1)
            pool.affine_select(out=ident[:, :], in_=ident[:, :], compare_op=ALU.not_equal, fill=1.0,
                               base=0, pattern=[[-1, P]], channel_multiplier=1).then_inc(sem("ident"), 1)
            pool.memset(neg_half[:, :], -0.5).then_inc(sem("halves"), 1)
            pool.iota(steps[:, :], pattern=[[-1, P]], base=-1, channel_multiplier=1).then_inc(sem("mask"), 1)
            pool.wait_ge(sem("mask"), 1)
            pool.tensor_scalar(expo[:, :], steps[:, :], 0.0, None, ALU.max).then_inc(sem("mask"), 1)
            pool.memset(decay_full[:, :], 1.0).then_inc(sem("mask"), 1)
            pool.wait_ge(sem("mask"), 3)
            pool.wait_ge(sem("sigmoid"), 1)
            pool.tensor_scalar(decay_full[:, :], decay_full[:, :], sig[:, 0:1], None, ALU.mult).then_inc(sem("mask"), 1)
            pool.wait_ge(sem("mask"), 4)
            pool.tensor_tensor(decay_mask[:, :], decay_full[:, :], expo[:, :], ALU.pow).then_inc(sem("mask"), 1)
            pool.wait_ge(sem("mask"), 5)
            pool.affine_select(out=decay_mask[:, :], in_=decay_mask[:, :], compare_op=ALU.is_gt, fill=0.0,
                               base=0, pattern=[[-1, P]], channel_multiplier=1).then_inc(sem("decays"), 1)
            pool.iota(steps[:, :], pattern=[[-1, P]], base=P - 1, channel_multiplier=0).then_inc(sem("mask"), 1)
            pool.wait_ge(sem("mask"), 6)
            pool.tensor_copy(expo[:, :], steps[:, :]).then_inc(sem("mask"), 1)
            pool.wait_ge(sem("mask"), 7)
            pool.tensor_tensor(decay_out[:, :], decay_full[:, :], expo[:, :], ALU.pow).then_inc(sem("decays"), 1)
            pool.iota(steps[:, 0:1], pattern=[[0, 1]], base=0, channel_multiplier=1).then_inc(sem("mask"), 1)
            pool.memset(decay_exps[:, 1:2], float(P)).then_inc(sem("mask"), 1)
            pool.wait_ge(sem("mask"), 9)
            pool.tensor_copy(decay_exps[:, 0:1], steps[:, 0:1]).then_inc(sem("mask"), 1)
            pool.wait_ge(sem("mask"), 10)
            pool.tensor_tensor(decay_cols[:, 0:2], decay_full[:, 0:2], decay_exps[:, 0:2], ALU.pow)\
                .then_inc(sem("decays"), 1)
            pool.wait_ge(sem("halves"), 1)
            for p in range(PAIRS):
                pool_front(pool, 0, 0, p)
                if p == AT_COARSE:
                    gather(pool, 1, 1)
            pool_sequence(pool, 0, 0, True)
            with pool.Fori(0, (BATCHES - 4) // 2) as i:
                pool_sequence(pool, i * 2 + 1, 1, True)
                pool_sequence(pool, i * 2 + 2, 0, True)
            pool_sequence(pool, BATCHES - 3, 1, True)
            pool_sequence(pool, BATCHES - 2, 0, True)
            pool_sequence(pool, BATCHES - 1, 1, False)


def kernel(x, L0_tok_fine_embed_w, L0_tok_coarse_embed_w, L0_tok_loc_to_cluster_w, L0_tok_loc_to_cluster_b,
           L0_attn_basis, L0_attn_q_coeffs, L0_attn_k_coeffs, L0_attn_v_coeffs, L0_attn_o_coeffs,
           L0_attn_decay_logit, L0_attn_mem_out_scale, L0_attn_read_coeffs, L0_attn_write_coeffs,
           L0_attn_channel_mix, L0_attn_bias, L0_attn_op_out_scale, L0_attn_mem_scale, L0_attn_op_scale,
           L0_ffn_router_w, L0_ffn_bias, L0_ffn_shared_w_gate, L0_ffn_shared_w_up, L0_ffn_shared_w_down,
           L0_ffn_w_gate, L0_ffn_w_up, L0_ffn_w_down):
    import numpy as np
    import concourse.bacc as bacc
    from concourse.bass_utils import run_bass_kernel_spmd as run

    def a(v):
        return np.asarray(v)

    def in_rows(routed, shared):
        both = np.concatenate([a(routed), a(shared)], axis=0)
        return both.transpose(2, 0, 1).reshape(D, PAIRS, 2 * F)

    def down_rows(routed, shared):
        both = np.concatenate([a(routed), a(shared)], axis=0)
        return both.reshape(PAIRS, 2, D, F).transpose(1, 3, 0, 2).reshape(2 * F, PAIRS, D)

    laid_out = {
        "ids": a(x).reshape(BATCHES * TILES, P).T,
        "table": np.concatenate([a(L0_tok_fine_embed_w), a(L0_tok_loc_to_cluster_w).T], axis=1),
        "cluster_b": a(L0_tok_loc_to_cluster_b).reshape(1, CLUSTERS),
        "coarse_w": a(L0_tok_coarse_embed_w),
        "basis_t": a(L0_attn_basis).T,
        "q_c": a(L0_attn_q_coeffs), "k_c": a(L0_attn_k_coeffs),
        "v_c": a(L0_attn_v_coeffs), "o_c": a(L0_attn_o_coeffs),
        "read_t": a(L0_attn_read_coeffs).T, "write_t": a(L0_attn_write_coeffs).T,
        "mix": a(L0_attn_channel_mix), "bias": a(L0_attn_bias).reshape(C, 1),
        "decay_logit": a(L0_attn_decay_logit).reshape(1, 1),
        "mem_out_scale": a(L0_attn_mem_out_scale).reshape(1, 1),
        "op_out_scale": a(L0_attn_op_out_scale).reshape(1, 1),
        "mem_scale": a(L0_attn_mem_scale).reshape(1, 1),
        "op_scale": a(L0_attn_op_scale).reshape(1, 1),
        "router_t": a(L0_ffn_router_w).T, "router_b": a(L0_ffn_bias).reshape(1, EXPERTS),
        "gate_t": in_rows(L0_ffn_w_gate, L0_ffn_shared_w_gate),
        "up_t": in_rows(L0_ffn_w_up, L0_ffn_shared_w_up),
        "down_t": down_rows(L0_ffn_w_down, L0_ffn_shared_w_down),
    }
    nc = bacc.Bacc("TRN2", target_bir_lowering=False, num_devices=1)
    arrays, args = {}, []
    for name, v in laid_out.items():
        v = np.ascontiguousarray(v)
        arrays[name + "_dram"] = v
        args.append(nc.dram_tensor(name + "_dram", v.shape, mybir.dt.from_np(v.dtype), kind="ExternalInput").ap())
    args.append(nc.dram_tensor("out_dram", (BATCHES, SEQ, D), F32, kind="ExternalOutput").ap())
    build(nc, *args)
    return run(nc, [arrays], core_ids=[0]).results[0]["out_dram"]
```

```python
from contextlib import ExitStack

import concourse.bass as bass
from concourse import mybir

F32 = mybir.dt.float32
F32R = mybir.dt.float32r
I32 = mybir.dt.int32
ALU = mybir.AluOpType
ACT = mybir.ActivationFunctionType
AX = mybir.AxisListType

P = 128
BATCHES, SEQ = 8, 512
TILES = SEQ // P
HALF = 64
CLUSTERS = 64
D = 128
C = 128
EXPERTS, F, TOP = 64, 64, 6
SHARED = 2
CAPACITY = int(BATCHES * SEQ * TOP * 2.0 / EXPERTS)
ROUTED_PAIRS = EXPERTS // 2
PAIRS = ROUTED_PAIRS + SHARED // 2
RMS_EPS, LN_EPS, GATE_EPS = 1.1920929e-07, 1e-05, 1e-09
SENTINEL = 2.0
RING = 3
GATE_RING = 4
LAG = 3

GATHER_AT = (1, 2, 3, 4)
DVE_AT = dict(xn=0, x1=2, xn_dec=3, y_dec=4, scores=5, state=6, x2=8, result=9, logits=10, xn2=12,
              exp_sum=13, h=16, bn1=17, h2=18, bn3=19, mv1=20, x3=21, x3_lo=23, router=25, prob=27,
              top=28, chosen=29, gates=30, taken=31)
PE_AT = dict(xn_t=1, y=2, z=3, scores=4, state=5, mem=7, out=8, exp_t=12, xn2_t=13, vals=14, coarse=15,
             op=17, x3_t=22, router=24, chosen_t=29, gates_t=30)
ACT_AT = dict(xn_t=2, y_t=3, z=4, ffn_t=5, squares=9, squares2=10, cluster_exp=11, exp_t=13, xn2_t=14, vals=15,
              x3_hi=23, router_exp=26)
POOL_AT = dict(inv2=11, hx=13, inv3=20, inv1=22)
STORE_AT = 14

CHUNK = 11
CHUNKS = [(n, p0) for p0 in range(0, PAIRS, CHUNK) for n in ("gate", "up")] + \
    [("down", p0) for p0 in range(0, PAIRS, CHUNK)]
SPLIT_AT = [0, 1, 3, 4, 5, 7, 9, 10, 12]


def build(nc, ids, table, cluster_b, coarse_w, basis_t, q_c, k_c, v_c, o_c, read_t, write_t, mix, bias,
          decay_logit, mem_out_scale, op_out_scale, mem_scale, op_scale, router_t, router_b,
          gate_t, up_t, down_t, out):
    ctx = ExitStack()
    with ctx:
        def sb(name, shape, dt=F32):
            return ctx.enter_context(nc.sbuf_tensor(name, shape, dt))

        sems = {}

        def sem(name):
            if name not in sems:
                sems[name] = ctx.enter_context(nc.semaphore(name))
            return sems[name]

        idx = sb("idx", [P, BATCHES * TILES], I32)
        cluster_b_row = sb("cluster_b_row", [P, CLUSTERS])
        router_b_row = sb("router_b_row", [P, EXPERTS])
        coarse_sb = sb("coarse_sb", [CLUSTERS, HALF])
        basis = sb("basis", [P, D])
        small_w = {n: sb("w_" + n, [P, C]) for n in ("q", "k", "v", "o", "read", "write", "mix")}
        bias_col = sb("bias_col", [P, 1])
        scalars = sb("scalars", [P, 5])
        router_raw = sb("router_raw", [P, EXPERTS])
        router_hi = sb("router_hi", [P, EXPERTS], F32R)
        router_lo = sb("router_lo", [P, EXPERTS], F32R)

        w_hi = {n: sb(f"{n}_hi", [P, PAIRS, P], F32R) for n in ("gate", "up", "down")}
        w_lo = {n: sb(f"{n}_lo", [P, PAIRS, P], F32R) for n in ("gate", "up", "down")}

        ident = sb("ident", [P, P])
        steps = sb("steps", [P, P], I32)
        expo = sb("expo", [P, P])
        decay_full = sb("decay_full", [P, P])
        decay_mask = sb("decay_mask", [P, P])
        decay_out = sb("decay_out", [P, P])
        decay_cols = sb("decay_cols", [P, 3])
        decay_exps = sb("decay_exps", [P, 3])
        sig = sb("sig", [P, 1])
        mem_mul = sb("mem_mul", [P, 1])
        op_mul = sb("op_mul", [P, 1])
        neg_half = sb("neg_half", [P, 2 * TILES])
        ones_row = sb("ones_row", [EXPERTS, SEQ])
        qk_in = sb("qk_in", [P, P])
        vo_in = sb("vo_in", [P, P])
        qk_t = sb("qk_t", [P, P])
        vo_t = sb("vo_t", [P, P])
        qk_w = sb("qk_w", [P, P])
        vo_w = sb("vo_w", [P, P])
        read_e = sb("read_e", [P, P])
        read_s = sb("read_s", [P, P])
        read_stat = sb("read_stat", [P, 4])
        read_mix = sb("read_mix", [P, P])
        write_w = sb("write_w", [P, P])

        emb = [sb(f"emb{i}", [P, TILES, D]) for i in range(2)]
        lg = sb("lg", [P, TILES, CLUSTERS])
        lg2 = sb("lg2", [P, TILES, CLUSTERS])
        lge = sb("lge", [P, TILES, CLUSTERS])
        soft = sb("soft", [P, 3, TILES])
        lge_t = sb("lge_t", [CLUSTERS, SEQ])
        bn1 = sb("bn1", [P, TILES, 6])
        mv1 = sb("mv1", [P, TILES, 2])
        var1 = sb("var1", [P, 2, TILES])
        inv1 = sb("inv1", [P, 2, TILES])
        x1 = sb("x1", [P, TILES, D])
        xn = sb("xn", [P, TILES, D])
        xn_dec = sb("xn_dec", [P, TILES - 1, D])
        xn_t = sb("xn_t", [P, SEQ])
        y_t = sb("y_t", [P, SEQ])
        y_dec = sb("y_dec", [P, TILES - 1, P])
        z = sb("z", [P, TILES, D])
        scores = sb("scores", [P, TILES, P])
        state = sb("state", [P, TILES - 1, P])
        x2 = sb("x2", [P, TILES, D])
        x2_sq = sb("x2_sq", [P, TILES, D])
        ss2 = sb("ss2", [P, TILES])
        ms2 = sb("ms2", [P, TILES])
        inv2 = sb("inv2", [P, TILES])
        xn2, xn2_t, vals = xn, xn_t, y_t
        hx = sb("hx", [P, TILES, D])
        h2 = [sb(f"h2_{i}", [P, TILES, D]) for i in range(2)]
        bn3 = sb("bn3", [P, TILES, 6])
        mv3 = sb("mv3", [P, TILES, 2])
        var3 = sb("var3", [P, TILES])
        inv3 = sb("inv3", [P, TILES])
        x3 = xn
        x3_hi = [sb(f"x3_hi{i}", [P, SEQ], F32R) for i in range(2)]
        x3_lo = [sb(f"x3_lo{i}", [P, SEQ], F32R) for i in range(2)]
        rl = sb("rl", [P, TILES, EXPERTS])
        rl2 = sb("rl2", [P, TILES, EXPERTS])
        re = sb("re", [P, TILES, EXPERTS])
        rstat = sb("rstat", [P, 3, TILES])
        prob = sb("prob", [P, TILES, EXPERTS + 2])
        top8 = sb("top8", [P, TILES, 8])
        struck = sb("struck", [P, TILES, EXPERTS + 2])
        tstat = sb("tstat", [P, 3, TILES])
        chosen = sb("chosen", [P, TILES, EXPERTS])
        gate_n = sb("gate_n", [P, TILES, EXPERTS])
        gates = sb("gates", [P, TILES, EXPERTS])
        taken_end = sb("taken_end", [EXPERTS, 1])
        idx_now = sb("idx_now", [P, TILES], I32)
        taken = sb("taken", [EXPERTS, SEQ])
        gates_t = sb("gates_t", [EXPERTS, SEQ])
        gate_rows = sb("gate_rows", [P, GATE_RING, SEQ])
        hid = sb("hid", [P, RING, SEQ])
        raw = [b.rearrange("p r s -> p (r s)")[:, 0:CHUNK * P].rearrange("p (c d) -> p c d", c=CHUNK)
               for b in (hid[:, :, :], gate_rows[:, :, :])]
        hid_hi = sb("hid_hi", [P, RING, SEQ], F32R)
        hid_lo = sb("hid_lo", [P, RING, SEQ], F32R)
        ffn_t = sb("ffn_t", [P, SEQ])
        result = sb("result", [P, TILES, D])
        gates_dram = nc.dram_tensor("gates_dram", (BATCHES, EXPERTS, SEQ), F32, kind="Internal").ap()

        def bank(name):
            return ctx.enter_context(nc.psum_tensor(name, [P, 512], F32))

        bank_g = [bank(f"bank_g{i}") for i in range(2)]
        bank_u = [bank(f"bank_u{i}") for i in range(2)]
        bank_y = [bank(f"bank_y{i}") for i in range(2)]
        bank_f = [bank(f"bank_f{i}") for i in range(2)]

        def tiles(b):
            return b[:, :].rearrange("p (t d) -> p t d", t=TILES)

        def over(col, n):
            return col.unsqueeze(2).to_broadcast([P, TILES, n])

        out_v = out.rearrange("b (t p) d -> b p t d", p=P)

        block = ctx.enter_context(nc.Block())

        def alone(eng, name):
            eng.sem_inc(sem(name), 1)

        def wait(eng, name, value):
            if isinstance(value, int) and value <= 0:
                return
            eng.wait_ge(sem(name), value)

        def sequences(eng, one):
            one(0, 0, True, True)
            with eng.Fori(0, (BATCHES - 4) // 2) as i:
                one(i * 2 + 1, 1, True, True, i + 2)
                one(i * 2 + 2, 0, True, True, i + 3)
            one(BATCHES - 3, 1, True, True, (BATCHES - 1) // 2 + 1)
            one(BATCHES - 2, 0, True, False)
            one(BATCHES - 1, 1, False, False)

        def gate_row_loads(sp, b, r):
            slot = r % GATE_RING
            if r == 0:
                sp.wait_ge(sem("gates_stored"), 16 * b + 16)
                if isinstance(b, int) and b == 0:
                    sp.wait_ge(sem("split_lo"), len(CHUNKS))
            if r >= GATE_RING:
                sp.wait_ge(sem("gated"), PAIRS * b + r + 1 - GATE_RING + 1)
            elif not (isinstance(b, int) and b == 0):
                sp.wait_ge(sem("gated"), PAIRS * b + r + 1 - GATE_RING)
            for e in range(2):
                src = gates_dram[b, 2 * r + e:2 * r + e + 1, :] if isinstance(b, int) else \
                    gates_dram[bass.ds(b, 1), 2 * r + e, :]
                sp.dma_start(gate_rows[F * e:F * e + F, slot, :],
                             src.to_broadcast([F, SEQ])).then_inc(sem(f"gate_rows{slot}"), 16)

        def sync_sequence(sp, b, par, late, early, use=0):
            for p in range(PAIRS):
                if p:
                    gate_row_loads(sp, b, p - 1)
                if p == STORE_AT and not (isinstance(b, int) and b == 0):
                    store(sp, b - 1)
            if late:
                store_gates(sp, b + 1)

        def store_gates(sp, b):
            sp.wait_ge(sem("gates_t"), b + 1)
            dst = gates_dram[b] if isinstance(b, int) else \
                gates_dram[bass.ds(b, 1), :, :].rearrange("a e s -> (a e) s")
            sp.dma_start(dst, gates_t[:, :]).then_inc(sem("gates_stored"), 16)

        def store(sp, b):
            sp.wait_ge(sem("result"), b + 1)
            dst = out_v[b] if isinstance(b, int) else \
                out_v[bass.ds(b, 1), :, :, :].rearrange("a p t d -> (a p) t d")
            sp.dma_start(dst, result[:, :, :]).then_inc(sem("stored"), 16)

        @block.sync
        def _(sp):
            sp.dma_start(idx[:, :], ids).then_inc(sem("idx"), 16)
            sp.dma_start(cluster_b_row[:, :], cluster_b.to_broadcast([P, CLUSTERS])).then_inc(sem("cluster_b"), 16)
            sp.dma_start(coarse_sb[:, :], coarse_w).then_inc(sem("coarse_w"), 16)
            sources = {"gate": gate_t, "up": up_t, "down": down_t}

            def weights(k):
                n, p0 = CHUNKS[k]
                if k >= 2:
                    sp.wait_ge(sem("split_lo"), k - 1)
                sp.dma_start(raw[k % 2][:, :, :], sources[n][:, p0:p0 + CHUNK, :]).then_inc(sem(f"raw{k % 2}"), 16)

            sp.dma_start(basis[:, :], basis_t).then_inc(sem("small"), 16)
            for n, src in (("q", q_c), ("k", k_c), ("v", v_c), ("o", o_c),
                           ("read", read_t), ("write", write_t), ("mix", mix)):
                sp.dma_start(small_w[n][:, :], src).then_inc(sem("small"), 16)
            sp.dma_start(bias_col[:, :], bias).then_inc(sem("small"), 16)
            weights(0)
            weights(1)
            sp.dma_start(router_raw[:, :], router_t).then_inc(sem("router"), 16)
            sp.dma_start(router_b_row[:, :], router_b.to_broadcast([P, EXPERTS])).then_inc(sem("router"), 16)
            for k in range(2, len(CHUNKS)):
                weights(k)
            store_gates(sp, 0)
            sequences(sp, lambda *a: sync_sequence(sp, *a))
            store(sp, BATCHES - 1)
            sp.wait_ge(sem("stored"), 16 * BATCHES + 16)
            sp.wait_ge(sem("gates_stored"), 16 * BATCHES)

        def pe_late(pe, b, par, p, early):
            f0, f1 = bank_f
            if p == PE_AT["xn_t"]:
                pe.wait_ge(sem("xn"), b + 1)
                wait(pe, "gates_t", b)
                for t in range(TILES):
                    last = pe.transpose(f0[:, t * P:t * P + P], xn[:, t, :], ident[:, :])
                last.then_inc(sem("pe_xn_t"), 1)
            if p == PE_AT["y"]:
                pe.wait_ge(sem("xn_t"), b + 1)
                pe.matmul(f1[:, :], qk_w[:, :], xn_t[:, :], start=True, stop=True).then_inc(sem("pe_y"), 1)
            if p == PE_AT["z"]:
                for t in range(TILES):
                    last = pe.matmul(f0[:, t * P:t * P + P], xn_t[:, t * P:t * P + P], vo_w[:, :],
                                     start=(t == 0), stop=(t == TILES - 1), skip_group_check=True)
                last.then_inc(sem("pe_z"), 1)
            if p == PE_AT["scores"]:
                pe.wait_ge(sem("y_t"), b + 1)
                for t in range(TILES):
                    last = pe.matmul(f1[:, t * P:t * P + P], xn_t[:, t * P:t * P + P], y_t[:, t * P:t * P + P],
                                     start=(t == 0), stop=(t == TILES - 1), skip_group_check=True)
                last.then_inc(sem("pe_scores"), 1)
            if p == PE_AT["state"]:
                pe.wait_ge(sem("z"), b + 1)
                pe.wait_ge(sem("xn_dec"), b + 1)
                for t in range(1, TILES):
                    last = pe.matmul(f0[:, (t - 1) * P:t * P], xn_dec[:, t - 1, :], z[:, t, :],
                                     start=(t == 1), stop=(t == TILES - 1), skip_group_check=True)
                last.then_inc(sem("pe_state"), 1)
            if p == PE_AT["mem"]:
                pe.wait_ge(sem("scores"), b + 1)
                pe.wait_ge(sem("y_dec"), b + 1)
                pe.wait_ge(sem("state"), b + 1)
                for t in range(TILES):
                    last = pe.matmul(f1[:, t * P:t * P + P], scores[:, t, :], z[:, t, :],
                                     start=(t == 0), stop=(t == TILES - 1), skip_group_check=True)
                    if t < TILES - 1:
                        last = pe.matmul(f1[:, t * P:t * P + P], y_dec[:, t, :], state[:, t, :],
                                         start=False, stop=False, skip_group_check=True)
                last.then_inc(sem("pe_mem"), 1)
            if p == PE_AT["xn2_t"]:
                pe.wait_ge(sem("xn2"), b + 1)
                wait(pe, "result", b - 1)
                for t in range(TILES):
                    last = pe.transpose(f0[:, t * P:t * P + P], xn2[:, t, :], ident[:, :])
                last.then_inc(sem("pe_xn2_t"), 1)
            if p == PE_AT["vals"]:
                pe.wait_ge(sem("xn2_t"), b + 1)
                if early:
                    pe.wait_ge(sem("exp_t"), b + 2)
                pe.matmul(f1[:, :], read_mix[:, :], xn2_t[:, :], start=True, stop=True).then_inc(sem("pe_vals"), 1)
            if p == PE_AT["op"]:
                pe.wait_ge(sem("vals"), b + 1)
                if early:
                    pe.wait_ge(sem("h"), b + 2)
                for t in range(TILES):
                    last = pe.matmul(f0[:, t * P:t * P + P], vals[:, t * P:t * P + P], write_w[:, :],
                                     start=(t == 0), stop=(t == TILES - 1), skip_group_check=True)
                last.then_inc(sem("pe_op"), 1)
            if p == PE_AT["x3_t"]:
                pe.wait_ge(sem("x3"), b + 1)
                for t in range(TILES):
                    last = pe.transpose(f1[:, t * P:t * P + P], x3[:, t, :], ident[:, :])
                last.then_inc(sem("pe_x3_t"), 1)
            if p == PE_AT["router"]:
                pe.wait_ge(sem("x3_hi"), b + 1)
                pe.wait_ge(sem("x3_lo"), b + 1)
                for t in range(TILES):
                    c = slice(t * P, t * P + P)
                    o = f0[:, t * EXPERTS:(t + 1) * EXPERTS]
                    pe.matmul(o, x3_hi[par][:, c], router_hi[:, :], start=(t == 0), stop=False, skip_group_check=True)
                    pe.matmul(o, x3_lo[par][:, c], router_hi[:, :], start=False, stop=False, skip_group_check=True)
                    last = pe.matmul(o, x3_hi[par][:, c], router_lo[:, :], start=False, stop=(t == TILES - 1),
                                     skip_group_check=True)
                last.then_inc(sem("pe_router"), 1)
            if p == PE_AT["chosen_t"]:
                pe.wait_ge(sem("chosen"), b + 1)
                alone(pe, "pe_passed")
                for t in range(TILES):
                    last = pe.transpose(f1[0:EXPERTS, t * P:t * P + P], chosen[:, t, :], ident[:, :])
                last.then_inc(sem("pe_chosen_t"), 1)
            if p == PE_AT["gates_t"]:
                pe.wait_ge(sem("gates"), b + 1)
                alone(pe, "pe_passed")
                for t in range(TILES):
                    last = pe.transpose(f0[0:EXPERTS, t * P:t * P + P], gates[:, t, :], ident[:, :])
                last.then_inc(sem("pe_gates_t"), 1)

        def pe_early(pe, b, p):
            f0, f1 = bank_f
            if p == PE_AT["exp_t"]:
                pe.wait_ge(sem("cluster_exp"), b + 1)
                wait(pe, "x2", b)
                alone(pe, "pe_passed")
                for t in range(TILES):
                    last = pe.transpose(f1[0:CLUSTERS, t * P:t * P + P], lge[:, t, :], ident[:, :])
                last.then_inc(sem("pe_exp_t"), 1)
            if p == PE_AT["coarse"]:
                pe.wait_ge(sem("exp_t"), b + 1)
                for t in range(TILES):
                    last = pe.matmul(f0[:, t * HALF:t * HALF + HALF], lge_t[:, t * P:t * P + P], coarse_sb[:, :],
                                     start=(t == 0), stop=(t == TILES - 1), skip_group_check=True)
                last.then_inc(sem("pe_coarse"), 1)

        def down(pe, b, par, p):
            q = PAIRS * b + p
            if isinstance(b, int) and b == 0 and p == 0:
                pe.wait_ge(sem("split_hi"), len(CHUNKS))
                pe.wait_ge(sem("split_lo"), len(CHUNKS))
            pe.wait_ge(sem("hid_hi"), q + 1)
            pe.wait_ge(sem("hid_lo"), q + 1)
            s, y = p % RING, bank_y[par]
            pe.matmul(y[:, :], w_hi["down"][:, p, :], hid_hi[:, s, :], start=(p == 0), stop=False)
            pe.matmul(y[:, :], w_lo["down"][:, p, :], hid_hi[:, s, :], start=False, stop=False)
            pe.matmul(y[:, :], w_hi["down"][:, p, :], hid_lo[:, s, :], start=False,
                      stop=(p == PAIRS - 1)).then_inc(sem("down_done"), 1)

        def pe_out(pe, b):
            pe.wait_ge(sem("ffn_t"), b + 1)
            for t in range(TILES):
                last = pe.transpose(bank_f[0][:, t * P:t * P + P], ffn_t[:, t * P:t * P + P], ident[:, :])
            last.then_inc(sem("pe_out"), 1)

        def pe_sequence(pe, b, par, late, early, use=0):
            first = isinstance(b, int) and b == 0
            for p in range(PAIRS):
                q = PAIRS * b + p
                ring = (p + par) % 2
                for name, banks, freed in (("gate", bank_g, "silu"), ("up", bank_u, "up_used")):
                    wait(pe, freed, q - 1)
                    o = banks[ring][:, :]
                    pe.matmul(o, w_hi[name][:, p, :], x3_hi[par][:, :], start=True, stop=False)
                    pe.matmul(o, w_lo[name][:, p, :], x3_hi[par][:, :], start=False, stop=False)
                    pe.matmul(o, w_hi[name][:, p, :], x3_lo[par][:, :], start=False,
                              stop=True).then_inc(sem("pe_" + name), 1)
                if p >= LAG:
                    down(pe, b, par, p - LAG)
                elif not first:
                    down(pe, b - 1, 1 - par, p - LAG + PAIRS)
                if p == PE_AT["out"] and not first:
                    pe_out(pe, b - 1)
                if late:
                    pe_late(pe, b + 1, 1 - par, p, early)
                if early:
                    pe_early(pe, b + 2, p)

        @block.tensor
        def _(pe):
            f0, f1 = bank_f
            pe.wait_ge(sem("small"), 16 * 9)
            pe.matmul(f0[:, 0:P], small_w["q"][:, :], small_w["k"][:, :], start=True, stop=True)
            pe.matmul(f0[:, P:2 * P], small_w["v"][:, :], small_w["o"][:, :], start=True, stop=True,
                      skip_group_check=True)
            pe.matmul(f0[:, 2 * P:3 * P], small_w["read"][:, :], basis[:, :], start=True, stop=True,
                      skip_group_check=True)
            pe.matmul(f0[:, 3 * P:4 * P], small_w["write"][:, :], basis[:, :], start=True, stop=True,
                      skip_group_check=True).then_inc(sem("pe_prep"), 1)
            pe.wait_ge(sem("prep1"), 1)
            pe.matmul(f1[:, 0:P], qk_in[:, :], basis[:, :], start=True, stop=True)
            pe.matmul(f1[:, P:2 * P], vo_in[:, :], basis[:, :], start=True, stop=True,
                      skip_group_check=True).then_inc(sem("pe_prep"), 1)
            pe.wait_ge(sem("prep2"), 1)
            pe.matmul(f0[:, 0:P], qk_t[:, :], basis[:, :], start=True, stop=True, skip_group_check=True)
            pe.matmul(f0[:, P:2 * P], vo_t[:, :], basis[:, :], start=True, stop=True, skip_group_check=True)
            pe.matmul(f0[:, 2 * P:3 * P], read_s[:, :], small_w["mix"][:, :], start=True, stop=True,
                      skip_group_check=True).then_inc(sem("pe_prep"), 1)
            pe.wait_ge(sem("prep3"), 1)
            pe.wait_ge(sem("coarse_w"), 16)
            pe.wait_ge(sem("ident"), 2)
            for p in range(PAIRS):
                pe_early(pe, 0, p)
            for p in range(PAIRS):
                if p == PE_AT["router"]:
                    pe.wait_ge(sem("router_split"), 2)
                pe_late(pe, 0, 0, p, True)
                pe_early(pe, 1, p)
            pe.wait_ge(sem("split_lo"), 2 * PAIRS // CHUNK)
            pe.wait_ge(sem("split_hi"), 2 * PAIRS // CHUNK)
            sequences(pe, lambda *a: pe_sequence(pe, *a))
            last = BATCHES - 1
            for p in range(PAIRS - LAG, PAIRS):
                down(pe, last, 1, p)
            pe_out(pe, last)

        def act_late(act, b, par, p):
            f0, f1 = bank_f
            if p == ACT_AT["xn_t"]:
                act.wait_ge(sem("pe_xn_t"), b + 1)
                act.activation(xn_t[:, :], f0[:, :], ACT.Copy).then_inc(sem("xn_t"), 1)
            if p == ACT_AT["y_t"]:
                act.wait_ge(sem("pe_y"), b + 1)
                act.activation(y_t[:, :], f1[:, :], ACT.Copy).then_inc(sem("y_t"), 1)
            if p == ACT_AT["z"]:
                act.wait_ge(sem("pe_z"), b + 1)
                act.activation(z[:, :, :], tiles(f0), ACT.Copy).then_inc(sem("z"), 1)
            if p in (ACT_AT["squares"], ACT_AT["squares2"]):
                first = 0 if p == ACT_AT["squares"] else TILES // 2
                act.wait_ge(sem("x2"), b + 1)
                for t in range(first, first + TILES // 2):
                    act.activation(x2_sq[:, t, :], x2[:, t, :], ACT.Square,
                                   accum_out=ss2[:, t:t + 1]).then_inc(sem("x2_squares"), 1)
            if p == ACT_AT["xn2_t"]:
                act.wait_ge(sem("pe_xn2_t"), b + 1)
                act.activation(xn2_t[:, :], f0[:, :], ACT.Copy).then_inc(sem("xn2_t"), 1)
            if p == ACT_AT["vals"]:
                act.wait_ge(sem("pe_vals"), b + 1)
                act.activation(vals[:, :], f1[:, :], ACT.Gelu, bias=bias_col[:, 0:1]).then_inc(sem("vals"), 1)
            if p == ACT_AT["x3_hi"]:
                act.wait_ge(sem("pe_x3_t"), b + 1)
                act.activation(x3_hi[par][:, :], f1[:, :], ACT.Copy).then_inc(sem("x3_hi"), 1)
            if p == ACT_AT["router_exp"]:
                act.wait_ge(sem("router_logits"), b + 1)
                act.activation(re[:, :, :], rl2[:, :, :], ACT.Exp).then_inc(sem("router_exp"), 1)

        def act_early(act, b, p):
            if p == ACT_AT["cluster_exp"]:
                act.wait_ge(sem("cluster_logits"), b + 1)
                act.activation(lge[:, :, :], lg2[:, :, :], ACT.Exp).then_inc(sem("cluster_exp"), 1)
            if p == ACT_AT["exp_t"]:
                act.wait_ge(sem("pe_exp_t"), b + 1)
                act.activation(lge_t[:, :], bank_f[1][0:CLUSTERS, :], ACT.Copy).then_inc(sem("exp_t"), 1)

        def act_silu(act, b, par, p):
            q = PAIRS * b + p
            act.wait_ge(sem("pe_gate"), q + 1)
            if isinstance(b, int) and b == 0 and p == 0:
                act.wait_ge(sem("split_lo"), len(CHUNKS))
            wait(act, "hid_lo", q - RING + 1)
            act.activation(hid[:, p % RING, :], bank_g[(p + par) % 2][:, :], ACT.Silu).then_inc(sem("silu"), 1)

        def act_hi(act, b, p):
            q = PAIRS * b + p
            act.wait_ge(sem("gated"), q + 1)
            wait(act, "down_done", q - RING + 1)
            act.activation(hid_hi[:, p % RING, :], hid[:, p % RING, :], ACT.Copy).then_inc(sem("hid_hi"), 1)

        def act_copy_out(act, b, par):
            act.wait_ge(sem("down_done"), PAIRS * b + PAIRS)
            act.activation(ffn_t[:, :], bank_y[par][:, :], ACT.Copy).then_inc(sem("ffn_t"), 1)

        def act_sequence(act, b, par, late, early, use=0):
            first = isinstance(b, int) and b == 0
            for p in range(PAIRS):
                if p == ACT_AT["ffn_t"] and not first:
                    act_copy_out(act, b - 1, 1 - par)
                if late:
                    act_late(act, b + 1, 1 - par, p)
                if early:
                    act_early(act, b + 2, p)
                act_silu(act, b, par, p)
                if p:
                    act_hi(act, b, p - 1)
                elif not first:
                    act_hi(act, b - 1, PAIRS - 1)

        @block.scalar
        def _(act):
            act.wait_ge(sem("scalars"), 16 * 5)
            act.activation(sig[:, :], scalars[:, 0:1], ACT.Sigmoid).then_inc(sem("sigmoid"), 1)
            act.wait_ge(sem("read_shifted"), 1)
            act.activation(read_e[:, :], read_s[:, :], ACT.Exp, accum_out=read_stat[:, 1:2])\
               .then_inc(sem("read_exp"), 1)
            for p in range(PAIRS):
                act_early(act, 0, p)
            act.wait_ge(sem("router"), 32)
            act.activation(router_hi[:, :], router_raw[:, :], ACT.Copy).then_inc(sem("router_split"), 1)
            for p in range(PAIRS):
                act_late(act, 0, 0, p)
                act_early(act, 1, p)
                if p in SPLIT_AT:
                    k = SPLIT_AT.index(p)
                    n, p0 = CHUNKS[k]
                    act.wait_ge(sem(f"raw{k % 2}"), 16 * (k // 2 + 1))
                    act.activation(w_hi[n][:, p0:p0 + CHUNK, :], raw[k % 2][:, :, :], ACT.Copy)\
                       .then_inc(sem("split_hi"), 1)
            sequences(act, lambda *a: act_sequence(act, *a))
            last = BATCHES - 1
            act_hi(act, last, PAIRS - 1)
            act_copy_out(act, last, 1)

        def dve_late(dve, b, par, p):
            f0, f1 = bank_f
            if p == DVE_AT["xn"]:
                dve.wait_ge(sem("inv1"), b + 1)
                for t in range(TILES):
                    last = dve.tensor_scalar(xn[:, t, :], emb[par][:, t, :], mv1[:, t, 0:1], inv1[:, 1, t:t + 1],
                                             ALU.subtract, ALU.mult)
                last.then_inc(sem("xn"), 1)
            if p == DVE_AT["x1"]:
                for t in range(TILES):
                    last = dve.tensor_scalar(x1[:, t, :], emb[par][:, t, :], mv1[:, t, 0:1], inv1[:, 0, t:t + 1],
                                             ALU.subtract, ALU.mult)
                last.then_inc(sem("x1"), 1)
            if p == DVE_AT["xn_dec"]:
                dve.wait_ge(sem("xn"), b + 1)
                dve.tensor_scalar(xn_dec[:, :, :], xn[:, 1:TILES, :], decay_cols[:, 0:1], None, ALU.mult)\
                   .then_inc(sem("xn_dec"), 1)
            if p == DVE_AT["y_dec"]:
                dve.wait_ge(sem("y_t"), b + 1)
                dve.tensor_tensor(y_dec[:, :, :], y_t[:, 0:(TILES - 1) * P].rearrange("p (t d) -> p t d", d=P),
                                  decay_out[:, :].unsqueeze(1).to_broadcast([P, TILES - 1, P]), ALU.mult)\
                   .then_inc(sem("y_dec"), 1)
            if p == DVE_AT["scores"]:
                dve.wait_ge(sem("pe_scores"), b + 1)
                dve.tensor_tensor(scores[:, :, :], tiles(f1),
                                  decay_mask[:, :].unsqueeze(1).to_broadcast([P, TILES, P]), ALU.mult)\
                   .then_inc(sem("scores"), 1)
            if p == DVE_AT["state"]:
                dve.wait_ge(sem("pe_state"), b + 1)
                dve.tensor_copy(state[:, TILES - 2, :], f0[:, (TILES - 2) * P:(TILES - 1) * P])\
                   .then_inc(sem("state_part"), 1)
                for k, c in enumerate(range(TILES - 3, -1, -1)):
                    dve.wait_ge(sem("state_part"), (TILES - 2) * b + k + 1)
                    dve.scalar_tensor_tensor(state[:, c, :], state[:, c + 1, :], decay_cols[:, 1:2],
                                             f0[:, c * P:c * P + P], ALU.mult, ALU.add)\
                       .then_inc(sem("state_part" if c else "state"), 1)
            if p == DVE_AT["x2"]:
                dve.wait_ge(sem("pe_mem"), b + 1)
                dve.wait_ge(sem("x1"), b + 1)
                dve.scalar_tensor_tensor(x2[:, :, :], tiles(f1), mem_mul[:, 0:1], x1[:, :, :], ALU.mult, ALU.add)\
                   .then_inc(sem("x2"), 1)
            if p == DVE_AT["xn2"]:
                dve.wait_ge(sem("inv2"), b + 1)
                for t in range(TILES):
                    last = dve.tensor_scalar(xn2[:, t, :], x2[:, t, :], inv2[:, t:t + 1], None, ALU.mult)
                last.then_inc(sem("xn2"), 1)
            if p == DVE_AT["h2"]:
                dve.wait_ge(sem("pe_op"), b + 1)
                dve.wait_ge(sem("hx"), b + 1)
                dve.scalar_tensor_tensor(h2[par][:, :, :], tiles(f0), op_mul[:, 0:1], hx[:, :, :], ALU.mult, ALU.add)\
                   .then_inc(sem("h2"), 1)
            if p == DVE_AT["bn3"]:
                dve.wait_ge(sem("h2"), b + 1)
                for t in range(TILES):
                    dve.bn_stats(bn3[:, t, :], h2[par][:, t, :]).then_inc(sem("bn3"), 1)
                dve.wait_ge(sem("bn3"), TILES * b + TILES)
                alone(dve, "dve_passed")
                for t in range(TILES):
                    last = dve.bn_aggr(mv3[:, t, :], bn3[:, t, :])
                last.then_inc(sem("mv3"), 1)
                dve.wait_ge(sem("mv3"), b + 1)
                dve.tensor_scalar(var3[:, :], mv3[:, :, 1], LN_EPS, None, ALU.add).then_inc(sem("var3"), 1)
            if p == DVE_AT["x3"]:
                dve.wait_ge(sem("inv3"), b + 1)
                for t in range(TILES):
                    last = dve.tensor_scalar(x3[:, t, :], h2[par][:, t, :], mv3[:, t, 0:1], inv3[:, t:t + 1],
                                             ALU.subtract, ALU.mult)
                last.then_inc(sem("x3"), 1)
            if p == DVE_AT["x3_lo"]:
                dve.wait_ge(sem("x3_hi"), b + 1)
                dve.tensor_tensor(x3_lo[par][:, :], f1[:, :], x3_hi[par][:, :].bitcast(F32), ALU.subtract)\
                   .then_inc(sem("x3_lo"), 1)
            if p == DVE_AT["router"]:
                dve.wait_ge(sem("pe_router"), b + 1)
                dve.tensor_tensor(rl[:, :, :], f0[:, 0:TILES * EXPERTS].rearrange("p (t e) -> p t e", t=TILES),
                                  router_b_row[:, :].unsqueeze(1).to_broadcast([P, TILES, EXPERTS]), ALU.add)\
                   .then_inc(sem("rl"), 1)
                dve.wait_ge(sem("rl"), b + 1)
                dve.tensor_reduce(rstat[:, 0, :], rl[:, :, :], AX.X, ALU.max).then_inc(sem("rl_max"), 1)
                dve.wait_ge(sem("rl_max"), b + 1)
                dve.tensor_tensor(rl2[:, :, :], rl[:, :, :], over(rstat[:, 0, :], EXPERTS), ALU.subtract)\
                   .then_inc(sem("router_logits"), 1)
            if p == DVE_AT["prob"]:
                dve.wait_ge(sem("router_exp"), b + 1)
                dve.tensor_reduce(rstat[:, 1, :], re[:, :, :], AX.X, ALU.add).then_inc(sem("re_sum"), 1)
                dve.wait_ge(sem("re_sum"), b + 1)
                dve.reciprocal(rstat[:, 2, :], rstat[:, 1, :]).then_inc(sem("re_inv"), 1)
                dve.wait_ge(sem("re_inv"), b + 1)
                dve.tensor_tensor(prob[:, :, 2:], re[:, :, :], over(rstat[:, 2, :], EXPERTS), ALU.mult)\
                   .then_inc(sem("prob"), 1)
            if p == DVE_AT["top"]:
                dve.wait_ge(sem("prob"), b + 1)
                alone(dve, "dve_passed")
                for t in range(TILES):
                    dve.max(top8[:, t, :], prob[:, t, :]).then_inc(sem("top8"), 1)
                dve.wait_ge(sem("top8"), TILES * b + TILES)
                dve.tensor_reduce(tstat[:, 0, :], top8[:, :, 2:], AX.X, ALU.add).then_inc(sem("top_sum"), 1)
                dve.wait_ge(sem("top_sum"), b + 1)
                dve.tensor_scalar(tstat[:, 1, :], tstat[:, 0, :], GATE_EPS, None, ALU.add).then_inc(sem("top_eps"), 1)
            if p == DVE_AT["chosen"]:
                for t in range(TILES):
                    last = dve.match_replace(struck[:, t, :], top8[:, t, :], prob[:, t, :], -1.0)
                last.then_inc(sem("struck"), 1)
                dve.wait_ge(sem("struck"), b + 1)
                dve.tensor_scalar(chosen[:, :, :], struck[:, :, 2:], 0.0, None, ALU.is_lt).then_inc(sem("chosen"), 1)
                dve.wait_ge(sem("top_eps"), b + 1)
                dve.reciprocal(tstat[:, 2, :], tstat[:, 1, :]).then_inc(sem("top_inv"), 1)
            if p == DVE_AT["gates"]:
                dve.wait_ge(sem("top_inv"), b + 1)
                dve.tensor_tensor(gate_n[:, :, :], prob[:, :, 2:], over(tstat[:, 2, :], EXPERTS), ALU.mult)\
                   .then_inc(sem("gate_n"), 1)
                dve.wait_ge(sem("gate_n"), b + 1)
                dve.wait_ge(sem("chosen"), b + 1)
                dve.tensor_tensor(gates[:, :, :], gate_n[:, :, :], chosen[:, :, :], ALU.mult).then_inc(sem("gates"), 1)
            if p == DVE_AT["taken"]:
                first = isinstance(b, int) and b == 0
                if not first:
                    dve.wait_ge(sem("taken"), b)
                    dve.tensor_copy(taken_end[:, :], taken[:, SEQ - 1:SEQ]).then_inc(sem("taken_end"), 1)
                    dve.wait_ge(sem("taken_end"), b)
                dve.wait_ge(sem("pe_chosen_t"), b + 1)
                dve.tensor_tensor_scan(taken[:, :], ones_row[:, :], f1[0:EXPERTS, :],
                                       0.0 if first else taken_end[:, :], ALU.mult, ALU.add)\
                   .then_inc(sem("taken"), 1)
                dve.wait_ge(sem("taken"), b + 1)
                dve.wait_ge(sem("pe_gates_t"), b + 1)
                wait(dve, "gates_stored", 16 * b)
                dve.scalar_tensor_tensor(gates_t[:, :], taken[:, :], float(CAPACITY), f0[0:EXPERTS, :],
                                         ALU.is_le, ALU.mult).then_inc(sem("gates_t"), 1)

        def dve_early(dve, b, par, p, use):
            e = emb[par]
            if p == DVE_AT["logits"]:
                dve.wait_ge(sem(f"gathered{par}"), 16 * TILES * use)
                dve.tensor_tensor(lg[:, :, :], e[:, :, HALF:D],
                                  cluster_b_row[:, :].unsqueeze(1).to_broadcast([P, TILES, CLUSTERS]),
                                  ALU.add).then_inc(sem("lg"), 1)
                dve.wait_ge(sem("lg"), b + 1)
                dve.tensor_reduce(soft[:, 0, :], lg[:, :, :], AX.X, ALU.max).then_inc(sem("lg_max"), 1)
                dve.wait_ge(sem("lg_max"), b + 1)
                dve.tensor_tensor(lg2[:, :, :], lg[:, :, :], over(soft[:, 0, :], CLUSTERS), ALU.subtract)\
                   .then_inc(sem("cluster_logits"), 1)
            if p == DVE_AT["exp_sum"]:
                dve.wait_ge(sem("cluster_exp"), b + 1)
                dve.tensor_reduce(soft[:, 1, :], lge[:, :, :], AX.X, ALU.add).then_inc(sem("lg_sum"), 1)
                dve.wait_ge(sem("lg_sum"), b + 1)
                dve.reciprocal(soft[:, 2, :], soft[:, 1, :]).then_inc(sem("lg_inv"), 1)
            if p == DVE_AT["h"]:
                dve.wait_ge(sem("pe_coarse"), b + 1)
                dve.wait_ge(sem("lg_inv"), b + 1)
                dve.tensor_tensor(e[:, :, HALF:D], bank_f[0][:, 0:TILES * HALF].rearrange("p (t d) -> p t d", t=TILES),
                                  over(soft[:, 2, :], HALF), ALU.mult).then_inc(sem("h"), 1)
            if p == DVE_AT["bn1"]:
                dve.wait_ge(sem("h"), b + 1)
                for t in range(TILES):
                    dve.bn_stats(bn1[:, t, :], e[:, t, :]).then_inc(sem("bn1"), 1)
            if p == DVE_AT["mv1"]:
                dve.wait_ge(sem("bn1"), TILES * b + TILES)
                alone(dve, "dve_passed")
                for t in range(TILES):
                    last = dve.bn_aggr(mv1[:, t, :], bn1[:, t, :])
                last.then_inc(sem("mv1"), 1)
                dve.wait_ge(sem("mv1"), b + 1)
                dve.tensor_scalar(var1[:, 0, :], mv1[:, :, 1], LN_EPS, None, ALU.add)
                dve.tensor_scalar(var1[:, 1, :], mv1[:, :, 1], 1.0 + RMS_EPS, RMS_EPS * LN_EPS, ALU.mult, ALU.add)\
                   .then_inc(sem("var1"), 1)

        def dve_up(dve, b, par, p):
            q = PAIRS * b + p
            dve.wait_ge(sem("silu"), q + 1)
            dve.wait_ge(sem("pe_up"), q + 1)
            s = p % RING
            dve.tensor_tensor(hid[:, s, :], hid[:, s, :], bank_u[(p + par) % 2][:, :], ALU.mult)\
               .then_inc(sem("up_used"), 1)

        def dve_lo(dve, b, p):
            q = PAIRS * b + p
            dve.wait_ge(sem("hid_hi"), q + 1)
            s = p % RING
            dve.tensor_tensor(hid_lo[:, s, :], hid[:, s, :], hid_hi[:, s, :].bitcast(F32), ALU.subtract)\
               .then_inc(sem("hid_lo"), 1)

        def dve_out(dve, b, par):
            dve.wait_ge(sem("pe_out"), b + 1)
            dve.wait_ge(sem("stored"), 16 * b + 16)
            dve.tensor_tensor(result[:, :, :], tiles(bank_f[0]), h2[par][:, :, :], ALU.add).then_inc(sem("result"), 1)

        def dve_sequence(dve, b, par, late, early, use=2):
            first = isinstance(b, int) and b == 0
            for p in range(PAIRS):
                if p == DVE_AT["result"] and not first:
                    dve_out(dve, b - 1, 1 - par)
                if late:
                    dve_late(dve, b + 1, 1 - par, p)
                if early:
                    dve_early(dve, b + 2, par, p, use)
                dve_up(dve, b, par, p)
                if p:
                    dve_lo(dve, b, p - 1)
                elif not first:
                    dve_lo(dve, b - 1, PAIRS - 1)

        @block.vector
        def _(dve):
            dve.sem_inc(sem("stored"), 16)
            dve.memset(ones_row[:, :], 1.0).then_inc(sem("ones"), 1)
            dve.memset(prob[:, :, 0:2], SENTINEL).then_inc(sem("sentinel"), 1)
            dve.wait_ge(sem("cluster_b"), 16)
            dve.wait_ge(sem("pe_prep"), 1)
            dve.tensor_reduce(read_stat[:, 0:1], bank_f[0][:, 2 * P:3 * P], AX.X, ALU.max).then_inc(sem("read_max"), 1)
            dve.tensor_copy(qk_in[:, :], bank_f[0][:, 0:P])
            dve.tensor_copy(vo_in[:, :], bank_f[0][:, P:2 * P])
            dve.tensor_copy(write_w[:, :], bank_f[0][:, 3 * P:4 * P]).then_inc(sem("prep1"), 1)
            dve.wait_ge(sem("read_max"), 1)
            dve.tensor_scalar(read_s[:, :], bank_f[0][:, 2 * P:3 * P], read_stat[:, 0:1], None, ALU.subtract)\
               .then_inc(sem("read_shifted"), 1)
            dve.wait_ge(sem("pe_prep"), 2)
            dve.tensor_copy(qk_t[:, :], bank_f[1][:, 0:P])
            dve.tensor_copy(vo_t[:, :], bank_f[1][:, P:2 * P])
            dve.wait_ge(sem("read_exp"), 1)
            dve.reciprocal(read_stat[:, 2:3], read_stat[:, 1:2]).then_inc(sem("read_inv"), 1)
            dve.wait_ge(sem("read_inv"), 1)
            dve.tensor_scalar(read_s[:, :], read_e[:, :], read_stat[:, 2:3], None, ALU.mult).then_inc(sem("prep2"), 1)
            dve.wait_ge(sem("pe_prep"), 3)
            dve.tensor_copy(qk_w[:, :], bank_f[0][:, 0:P])
            dve.tensor_copy(vo_w[:, :], bank_f[0][:, P:2 * P])
            dve.tensor_copy(read_mix[:, :], bank_f[0][:, 2 * P:3 * P]).then_inc(sem("prep3"), 1)
            dve.wait_ge(sem("scalars"), 16 * 5)
            dve.tensor_tensor(mem_mul[:, :], scalars[:, 1:2], scalars[:, 3:4], ALU.mult).then_inc(sem("muls"), 1)
            dve.tensor_tensor(op_mul[:, :], scalars[:, 2:3], scalars[:, 4:5], ALU.mult).then_inc(sem("muls"), 1)
            dve.wait_ge(sem("sentinel"), 1)
            dve.wait_ge(sem("ones"), 1)
            dve.wait_ge(sem("muls"), 2)
            for p in range(PAIRS):
                dve_early(dve, 0, 0, p, 1)
            dve.wait_ge(sem("router_split"), 1)
            dve.tensor_tensor(router_lo[:, :], router_raw[:, :], router_hi[:, :].bitcast(F32), ALU.subtract)\
               .then_inc(sem("router_split"), 1)
            dve.wait_ge(sem("decays"), 3)
            for p in range(PAIRS):
                dve_late(dve, 0, 0, p)
                dve_early(dve, 1, 1, p, 1)
                if p in SPLIT_AT:
                    k = SPLIT_AT.index(p)
                    n, p0 = CHUNKS[k]
                    dve.wait_ge(sem("split_hi"), k + 1)
                    dve.tensor_tensor(w_lo[n][:, p0:p0 + CHUNK, :], raw[k % 2][:, :, :],
                                      w_hi[n][:, p0:p0 + CHUNK, :].bitcast(F32), ALU.subtract)\
                       .then_inc(sem("split_lo"), 1)
            sequences(dve, lambda *a: dve_sequence(dve, *a))
            last = BATCHES - 1
            dve_lo(dve, last, PAIRS - 1)
            dve_out(dve, last, 1)

        def gather(pool, b, par, t, prev_use):
            if isinstance(b, int):
                at = idx[:, b * TILES + t:b * TILES + t + 1]
            else:
                at = idx_now[:, t:t + 1]
            if t == 0:
                wait(pool, "hx", b - 1)
                if not isinstance(b, int):
                    pool.wait_ge(sem(f"gathered{1 - par}"), 16 * TILES * prev_use)
                    pool.tensor_copy(idx_now[:, :], idx[:, bass.ds(b * TILES, TILES)]).then_inc(sem("idx_now"), 1)
                    pool.wait_ge(sem("idx_now"), b - 2)
                alone(pool, "pool_passed")
            pool.indirect_dma_start(emb[par][:, t, :], None, table[:, :],
                                    bass.IndirectOffsetOnAxis(ap=at, axis=0)).then_inc(sem(f"gathered{par}"), 16)

        def pool_late(pool, b, par, p):
            if p == POOL_AT["inv2"]:
                pool.wait_ge(sem("x2_squares"), TILES * b + TILES)
                alone(pool, "pool_passed")
                pool.tensor_scalar(ms2[:, :], ss2[:, :], 1.0 / D, RMS_EPS, ALU.mult, ALU.add).then_inc(sem("ms2"), 1)
                pool.wait_ge(sem("ms2"), b + 1)
                pool.tensor_tensor(inv2[:, :], ms2[:, :], neg_half[:, 0:TILES], ALU.pow).then_inc(sem("inv2"), 1)
            if p == POOL_AT["hx"]:
                pool.wait_ge(sem("x2"), b + 1)
                pool.tensor_tensor(hx[:, :, :], emb[par][:, :, :], x2[:, :, :], ALU.add).then_inc(sem("hx"), 1)
            if p == POOL_AT["inv3"]:
                pool.wait_ge(sem("var3"), b + 1)
                pool.tensor_tensor(inv3[:, :], var3[:, :], neg_half[:, 0:TILES], ALU.pow).then_inc(sem("inv3"), 1)

        def pool_early(pool, b, p):
            if p == POOL_AT["inv1"]:
                pool.wait_ge(sem("var1"), b + 1)
                pool.tensor_tensor(inv1[:, :, :], var1[:, :, :], neg_half[:, :].rearrange("p (k t) -> p k t", k=2),
                                   ALU.pow).then_inc(sem("inv1"), 1)

        def pool_sequence(pool, b, par, late, early, use=0):
            for p in range(PAIRS):
                if late:
                    pool_late(pool, b + 1, 1 - par, p)
                if early:
                    pool_early(pool, b + 2, p)
                    if p in GATHER_AT:
                        gather(pool, b + 2, par, GATHER_AT.index(p), use if par else use - 1)
                q = PAIRS * b + p
                s = p % RING
                pool.wait_ge(sem("up_used"), q + 1)
                if p:
                    slot, uses = (p - 1) % GATE_RING, ROUTED_PAIRS // GATE_RING
                    pool.wait_ge(sem(f"gate_rows{slot}"), 32 * uses * b + 32 * ((p - 1) // GATE_RING + 1))
                    pool.tensor_tensor(hid[:, s, :], hid[:, s, :], gate_rows[:, slot, :], ALU.mult)\
                        .then_inc(sem("gated"), 1)
                else:
                    alone(pool, "pool_passed")
                    pool.tensor_scalar(hid[:, s, :], hid[:, s, :], 1.0 / SHARED, None, ALU.mult)\
                        .then_inc(sem("gated"), 1)

        @block.gpsimd
        def _(pool):
            pool.wait_ge(sem("idx"), 16)
            for t in range(TILES):
                gather(pool, 0, 0, t, 0)
            for k, src in enumerate((decay_logit, mem_out_scale, op_out_scale, mem_scale, op_scale)):
                pool.dma_start(scalars[:, k:k + 1], src.to_broadcast([P, 1])).then_inc(sem("scalars"), 16)
            pool.memset(ident[:, :], 0.0).then_inc(sem("ident"), 1)
            pool.wait_ge(sem("ident"), 1)
            pool.affine_select(out=ident[:, :], in_=ident[:, :], compare_op=ALU.not_equal, fill=1.0,
                               base=0, pattern=[[-1, P]], channel_multiplier=1).then_inc(sem("ident"), 1)
            pool.memset(neg_half[:, :], -0.5).then_inc(sem("halves"), 1)
            pool.iota(steps[:, :], pattern=[[-1, P]], base=-1, channel_multiplier=1).then_inc(sem("mask"), 1)
            pool.wait_ge(sem("mask"), 1)
            pool.tensor_scalar(expo[:, :], steps[:, :], 0.0, None, ALU.max).then_inc(sem("mask"), 1)
            pool.memset(decay_full[:, :], 1.0).then_inc(sem("mask"), 1)
            pool.wait_ge(sem("mask"), 3)
            pool.wait_ge(sem("sigmoid"), 1)
            pool.tensor_scalar(decay_full[:, :], decay_full[:, :], sig[:, 0:1], None, ALU.mult).then_inc(sem("mask"), 1)
            pool.wait_ge(sem("mask"), 4)
            pool.tensor_tensor(decay_mask[:, :], decay_full[:, :], expo[:, :], ALU.pow).then_inc(sem("mask"), 1)
            pool.wait_ge(sem("mask"), 5)
            pool.affine_select(out=decay_mask[:, :], in_=decay_mask[:, :], compare_op=ALU.is_gt, fill=0.0,
                               base=0, pattern=[[-1, P]], channel_multiplier=1).then_inc(sem("decays"), 1)
            pool.iota(steps[:, :], pattern=[[-1, P]], base=P - 1, channel_multiplier=0).then_inc(sem("mask"), 1)
            pool.wait_ge(sem("mask"), 6)
            pool.tensor_copy(expo[:, :], steps[:, :]).then_inc(sem("mask"), 1)
            pool.wait_ge(sem("mask"), 7)
            pool.tensor_tensor(decay_out[:, :], decay_full[:, :], expo[:, :], ALU.pow).then_inc(sem("decays"), 1)
            pool.iota(steps[:, 0:1], pattern=[[0, 1]], base=0, channel_multiplier=1).then_inc(sem("mask"), 1)
            pool.memset(decay_exps[:, 1:2], float(P)).then_inc(sem("mask"), 1)
            pool.wait_ge(sem("mask"), 9)
            pool.tensor_copy(decay_exps[:, 0:1], steps[:, 0:1]).then_inc(sem("mask"), 1)
            pool.wait_ge(sem("mask"), 10)
            pool.tensor_tensor(decay_cols[:, 0:2], decay_full[:, 0:2], decay_exps[:, 0:2], ALU.pow)\
                .then_inc(sem("decays"), 1)
            pool.wait_ge(sem("halves"), 1)
            for t in range(TILES):
                gather(pool, 1, 1, t, 0)
            for p in range(PAIRS):
                pool_early(pool, 0, p)
            for p in range(PAIRS):
                pool_late(pool, 0, 0, p)
                pool_early(pool, 1, p)
            sequences(pool, lambda *a: pool_sequence(pool, *a))


def kernel(x, L0_tok_fine_embed_w, L0_tok_coarse_embed_w, L0_tok_loc_to_cluster_w, L0_tok_loc_to_cluster_b,
           L0_attn_basis, L0_attn_q_coeffs, L0_attn_k_coeffs, L0_attn_v_coeffs, L0_attn_o_coeffs,
           L0_attn_decay_logit, L0_attn_mem_out_scale, L0_attn_read_coeffs, L0_attn_write_coeffs,
           L0_attn_channel_mix, L0_attn_bias, L0_attn_op_out_scale, L0_attn_mem_scale, L0_attn_op_scale,
           L0_ffn_router_w, L0_ffn_bias, L0_ffn_shared_w_gate, L0_ffn_shared_w_up, L0_ffn_shared_w_down,
           L0_ffn_w_gate, L0_ffn_w_up, L0_ffn_w_down):
    import numpy as np
    import concourse.bacc as bacc
    from concourse.bass_utils import run_bass_kernel_spmd as run

    def a(v):
        return np.asarray(v)

    def in_rows(routed, shared):
        both = np.concatenate([a(shared), a(routed)], axis=0)
        return both.transpose(2, 0, 1).reshape(D, PAIRS, 2 * F)

    def down_rows(routed, shared):
        both = np.concatenate([a(shared), a(routed)], axis=0)
        return both.reshape(PAIRS, 2, D, F).transpose(1, 3, 0, 2).reshape(2 * F, PAIRS, D)

    laid_out = {
        "ids": a(x).reshape(BATCHES * TILES, P).T,
        "table": np.concatenate([a(L0_tok_fine_embed_w), a(L0_tok_loc_to_cluster_w).T], axis=1),
        "cluster_b": a(L0_tok_loc_to_cluster_b).reshape(1, CLUSTERS),
        "coarse_w": a(L0_tok_coarse_embed_w),
        "basis_t": a(L0_attn_basis).T,
        "q_c": a(L0_attn_q_coeffs), "k_c": a(L0_attn_k_coeffs),
        "v_c": a(L0_attn_v_coeffs), "o_c": a(L0_attn_o_coeffs),
        "read_t": a(L0_attn_read_coeffs).T, "write_t": a(L0_attn_write_coeffs).T,
        "mix": a(L0_attn_channel_mix), "bias": a(L0_attn_bias).reshape(C, 1),
        "decay_logit": a(L0_attn_decay_logit).reshape(1, 1),
        "mem_out_scale": a(L0_attn_mem_out_scale).reshape(1, 1),
        "op_out_scale": a(L0_attn_op_out_scale).reshape(1, 1),
        "mem_scale": a(L0_attn_mem_scale).reshape(1, 1),
        "op_scale": a(L0_attn_op_scale).reshape(1, 1),
        "router_t": a(L0_ffn_router_w).T, "router_b": a(L0_ffn_bias).reshape(1, EXPERTS),
        "gate_t": in_rows(L0_ffn_w_gate, L0_ffn_shared_w_gate),
        "up_t": in_rows(L0_ffn_w_up, L0_ffn_shared_w_up),
        "down_t": down_rows(L0_ffn_w_down, L0_ffn_shared_w_down),
    }
    nc = bacc.Bacc("TRN2", target_bir_lowering=False, num_devices=1)
    arrays, args = {}, []
    for name, v in laid_out.items():
        v = np.ascontiguousarray(v)
        arrays[name + "_dram"] = v
        args.append(nc.dram_tensor(name + "_dram", v.shape, mybir.dt.from_np(v.dtype), kind="ExternalInput").ap())
    args.append(nc.dram_tensor("out_dram", (BATCHES, SEQ, D), F32, kind="ExternalOutput").ap())
    build(nc, *args)
    return run(nc, [arrays], core_ids=[0]).results[0]["out_dram"]
```

```python
from contextlib import ExitStack

import concourse.bass as bass
from concourse import mybir

F32 = mybir.dt.float32
F32R = mybir.dt.float32r
I32 = mybir.dt.int32
ALU = mybir.AluOpType
ACT = mybir.ActivationFunctionType
AX = mybir.AxisListType

P = 128
BATCHES, SEQ = 8, 512
TILES = SEQ // P
HALF = 64
CLUSTERS = 64
D = 128
C = 128
EXPERTS, F, TOP = 64, 64, 6
SHARED = 2
CAPACITY = int(BATCHES * SEQ * TOP * 2.0 / EXPERTS)
ROUTED_PAIRS = EXPERTS // 2
PAIRS = ROUTED_PAIRS + SHARED // 2
RMS_EPS, LN_EPS, GATE_EPS = 1.1920929e-07, 1e-05, 1e-09
SENTINEL = 2.0
RING = 6
GATE_RING = 4
LAG = 4
SPLIT_LAG = 2

GATHER_AT = (1, 2, 3, 4)
DVE_AT = dict(xn=0, xn_lo=2, x1=5, xn_dec=5, y_lo=4, scores=6, state=6, x2=8, result=10, logits=9, xn2=11, exp_sum=12,
              h=15, bn1=16, h2=17, bn3=17, mv1=18, x3=19, x3_lo=21, router=24, prob=26, top=27, chosen=28, gates=29,
              taken=31)
PE_AT = dict(xn_t=1, y=3, z_scores=5, state=6, mem=7, out=8, exp_t=11, xn2_t=12, vals=13, coarse=14, op=16, x3_t=20,
             router=23, gates_t=30)
ACT_AT = dict(xn_hi=2, y_hi=4, z=6, ffn_t=5, squares=9, squares2=10, cluster_exp=10, exp_t=12, xn2_t=13, vals=14,
              x3_hi=21, router_exp=24)
POOL_AT = dict(inv2=10, hx=12, inv3=18, inv1=20)
STORE_AT = 14

SQUARES = ("basis", "q", "k", "v", "o", "read", "write", "mix")
PREP = ("qk_in", "vo_in", "qk_t", "vo_t", "read_e", "read_s", "ones", "above", "mask_t", "powers_t", "to_end")

CHUNK = 11
CHUNKS = [(n, p0) for p0 in range(0, PAIRS, CHUNK) for n in ("gate", "up")] + \
    [("down", p0) for p0 in range(0, PAIRS, CHUNK)]
HI_AT = (-20, -20, -20, -20, 4, 5, 6, 12, 12)
LO_AT = (("pool", -10), ("vector", 0), ("pool", -10), ("vector", 0), ("pool", 0), ("vector", 6), ("vector", 8),
         ("pool", 14), ("vector", 14))
RAW_PARTS = 4
SHIFT = 3
AHEAD = 2


def build(nc, ids, table, coarse_w, square_w, small_cols, small_rows, gate_t, up_t, down_t, out):
    ctx = ExitStack()
    with ctx:
        def sb(name, shape, dt=F32):
            return ctx.enter_context(nc.sbuf_tensor(name, shape, dt))

        sems = {}

        def sem(name):
            if name not in sems:
                sems[name] = ctx.enter_context(nc.semaphore(name))
            return sems[name]

        idx = sb("idx", [P, BATCHES * TILES], I32)
        rows = sb("rows", [P, CLUSTERS + EXPERTS + 5])
        cluster_b_row = rows[:, 0:CLUSTERS]
        router_b_row = rows[:, CLUSTERS:CLUSTERS + EXPERTS]
        scalars = rows[:, CLUSTERS + EXPERTS:]
        coarse_sb = sb("coarse_sb", [CLUSTERS, HALF])
        cols = sb("cols", [P, EXPERTS + 1])
        router_w = cols[:, 0:EXPERTS]
        bias_col = cols[:, EXPERTS:]
        shared = sb("shared", [P, (len(SQUARES) + len(PREP)) * P])
        squares = shared[:, 0:len(SQUARES) * P]
        small_w = {n: squares[:, k * P:k * P + P] for k, n in enumerate(SQUARES)}
        basis = small_w["basis"]
        (qk_in, vo_in, qk_t, vo_t, read_e, read_s,
         ones,
         above,
         mask_t,
         powers_t,
         to_end
         ) = (shared[:, k * P:k * P + P] for k in range(len(SQUARES), len(SQUARES) + len(PREP)))
        x2, x2_sq, hx, scores = (shared[:, k * SEQ:k * SEQ + SEQ].rearrange("p (t d) -> p t d", t=TILES)
                                 for k in range(4))
        xn_dec = shared[:, 4 * SEQ:4 * SEQ + (TILES - 1) * P].rearrange("p (t d) -> p t d", t=TILES - 1)

        w_hi = {n: sb(f"{n}_hi", [P, PAIRS, P], F32R) for n in ("gate", "up", "down")}
        w_lo = {n: sb(f"{n}_lo", [P, PAIRS, P], F32R) for n in ("gate", "up", "down")}

        ident = sb("ident", [P, P])
        decay_full = sb("decay_full", [P, P])
        decay_mask = sb("decay_mask", [P, P])
        decay_out = sb("decay_out", [P, P])
        decay_cols = sb("decay_cols", [P, 2])
        sig = sb("sig", [P, 1])
        mem_mul = sb("mem_mul", [P, 1])
        op_mul = sb("op_mul", [P, 1])
        neg_half = sb("neg_half", [P, 2 * TILES])
        ones_row = sb("ones_row", [EXPERTS, SEQ])
        qk_hi = sb("qk_hi", [P, P], F32R)
        qk_lo = sb("qk_lo", [P, P], F32R)
        vo_y_hi = sb("vo_y_hi", [P, (1 + TILES) * P], F32R)
        vo_y_lo = sb("vo_y_lo", [P, (1 + TILES) * P], F32R)
        read_stat = sb("read_stat", [P, 4])
        read_mix = sb("read_mix", [P, P])
        write_w = sb("write_w", [P, P])

        emb = [sb(f"emb{i}", [P, TILES, D]) for i in range(2)]
        lg = sb("lg", [P, TILES, CLUSTERS])
        soft = sb("soft", [P, 3, TILES])
        bn1 = sb("bn1", [P, TILES, 6])
        mv1 = sb("mv1", [P, TILES, 2])
        var1 = sb("var1", [P, 2, TILES])
        inv1 = sb("inv1", [P, 2, TILES])
        x1 = sb("x1", [P, TILES, D])
        xn = sb("xn", [P, TILES, D])
        xn2_t = sb("xn2_t", [P, SEQ])
        vals = sb("vals", [P, SEQ])
        turns = sb("turns", [P, 2 * (TILES - 1) * P])
        y_dec, state = (turns[:, k * (TILES - 1) * P:(k + 1) * (TILES - 1) * P]
                        .rearrange("p (t d) -> p t d", t=TILES - 1) for k in range(2))
        z = sb("z", [P, TILES, D])
        lge_t = z[0:CLUSTERS, :, :].rearrange("p t d -> p (t d)")
        ss2 = sb("ss2", [P, TILES])
        ms2 = sb("ms2", [P, TILES])
        inv2 = sb("inv2", [P, TILES])
        xn2 = xn
        later = sb("later", [P, 3, SEQ])
        ffn_t = later[:, 0, :]
        result, h2_1 = (later[:, k, :].rearrange("p (t d) -> p t d", t=TILES) for k in (1, 2))
        h2 = [sb("h2_0", [P, TILES, D]), h2_1]
        bn3 = sb("bn3", [P, TILES, 6])
        mv3 = sb("mv3", [P, TILES, 2])
        var3 = sb("var3", [P, TILES])
        inv3 = sb("inv3", [P, TILES])
        x3, x3_t = xn, xn2_t
        x3_hi = [sb(f"x3_hi{i}", [P, SEQ], F32R) for i in range(2)]
        x3_lo = [sb(f"x3_lo{i}", [P, SEQ], F32R) for i in range(2)]
        xn_hi, xn_lo = x3_hi, x3_lo
        rl = turns[:, 0:TILES * EXPERTS].rearrange("p (t e) -> p t e", t=TILES)
        rstat = sb("rstat", [P, 3, TILES])
        prob = sb("prob", [P, TILES, EXPERTS + 2])
        top8 = sb("top8", [P, TILES, 8])
        struck = sb("struck", [P, TILES, EXPERTS + 2])
        tstat = sb("tstat", [P, 3, TILES])
        chosen_gates = turns[:, TILES * EXPERTS:3 * TILES * EXPERTS].rearrange("p (t e) -> p t e", t=TILES)
        chosen, gates = chosen_gates[:, :, 0:EXPERTS], chosen_gates[:, :, EXPERTS:]
        taken_end = sb("taken_end", [EXPERTS, 1])
        idx_now = sb("idx_now", [P, TILES], I32)
        taken = sb("taken", [EXPERTS, SEQ])
        gates_t = sb("gates_t", [EXPERTS, SEQ])
        gate_rows = sb("gate_rows", [P, GATE_RING, SEQ])
        hid = sb("hid", [P, RING, SEQ])
        hid_hi = sb("hid_hi", [P, RING, SEQ], F32R)
        hid_lo = sb("hid_lo", [P, RING, SEQ], F32R)
        raw = [b.rearrange("p r s -> p (r s)")[:, 0:CHUNK * P].rearrange("p (c d) -> p c d", c=CHUNK)
               for b in (hid[:, 0:RING // 2, :], gate_rows[:, :, :], hid[:, RING // 2:RING, :], later[:, :, :])]
        gates_dram = nc.dram_tensor("gates_dram", (BATCHES, EXPERTS, SEQ), F32, kind="Internal").ap()

        def bank(name):
            return ctx.enter_context(nc.psum_tensor(name, [P, 512], F32))

        bank_g = [bank(f"bank_g{i}") for i in range(2)]
        bank_u = [bank(f"bank_u{i}") for i in range(2)]
        bank_y = [bank(f"bank_y{i}") for i in range(2)]
        bank_f = [bank(f"bank_f{i}") for i in range(2)]

        def tiles(b):
            return b[:, :].rearrange("p (t d) -> p t d", t=TILES)

        def z_scores(k):
            return bank_f[k][:, :].rearrange("p (t j d) -> p t j d", t=2, j=2)

        def slot(par, p):
            return (p + PAIRS * par) % RING

        def over(col, n):
            return col.unsqueeze(2).to_broadcast([P, TILES, n])

        out_v = out.rearrange("b (t p) d -> b p t d", p=P)

        block = ctx.enter_context(nc.Block())

        def alone(eng, name):
            eng.sem_inc(sem(name), 1)

        def wait(eng, name, value):
            if isinstance(value, int) and value <= 0:
                return
            eng.wait_ge(sem(name), value)

        def sequences(eng, one):
            one(0, 0, True, True)
            with eng.Fori(0, (BATCHES - 4) // 2) as i:
                one(i * 2 + 1, 1, True, True, i + 2)
                one(i * 2 + 2, 0, True, True, i + 3)
            one(BATCHES - 3, 1, True, True, (BATCHES - 1) // 2 + 1)
            one(BATCHES - 2, 0, True, False)
            one(BATCHES - 1, 1, False, False)

        def weights_split(eng, chunks):
            for part in range(min(RAW_PARTS, chunks)):
                eng.wait_ge(sem(f"split_lo{part}"), (chunks - 1 - part) // RAW_PARTS + 1)

        def split_lo(eng, name, at):
            for k, (n, p0) in enumerate(CHUNKS):
                if LO_AT[k] == (name, at):
                    eng.wait_ge(sem("split_hi"), k + 1)
                    eng.tensor_tensor(w_lo[n][:, p0:p0 + CHUNK, :], raw[k % RAW_PARTS],
                                      w_hi[n][:, p0:p0 + CHUNK, :].bitcast(F32), ALU.subtract)\
                       .then_inc(sem(f"split_lo{k % RAW_PARTS}"), 1)

        def gate_row_loads(sp, b, r):
            row = r % GATE_RING
            if r == 0:
                sp.wait_ge(sem("gates_stored"), 16 * b + 16)
                if isinstance(b, int) and b == 0:
                    weights_split(sp, len(CHUNKS))
            if r >= GATE_RING:
                sp.wait_ge(sem("gated"), PAIRS * b + r + 1 - GATE_RING + 1)
            elif not (isinstance(b, int) and b == 0):
                sp.wait_ge(sem("gated"), PAIRS * b + r + 1 - GATE_RING)
            src = gates_dram[b, 2 * r:2 * r + 2, :] if isinstance(b, int) else \
                gates_dram[bass.ds(b, 1), 2 * r:2 * r + 2, :].rearrange("a e s -> (a e) s")
            sp.dma_start(gate_rows[:, row, :],
                         src.unsqueeze(1).to_broadcast([2, F, SEQ])).then_inc(sem(f"gate_rows{row}"), 16)

        def sync_sequence(sp, b, par, late, early, use=0):
            for p in range(PAIRS):
                if p:
                    gate_row_loads(sp, b, p - 1)
                if p == STORE_AT and not (isinstance(b, int) and b == 0):
                    store(sp, b - 1)
            if late:
                store_gates(sp, b + 1)

        def store_gates(sp, b):
            sp.wait_ge(sem("gates_t"), b + 1)
            dst = gates_dram[b] if isinstance(b, int) else \
                gates_dram[bass.ds(b, 1), :, :].rearrange("a e s -> (a e) s")
            sp.dma_start(dst, gates_t[:, :]).then_inc(sem("gates_stored"), 16)

        def store(sp, b):
            sp.wait_ge(sem("result"), b + 1)
            dst = out_v[b] if isinstance(b, int) else \
                out_v[bass.ds(b, 1), :, :, :].rearrange("a p t d -> (a p) t d")
            sp.dma_start(dst, result[:, :, :]).then_inc(sem("stored"), 16)

        @block.sync
        def _(sp):
            sp.dma_start(idx[:, :], ids).then_inc(sem("idx"), 16)
            sp.dma_start(rows[:, :], small_rows.to_broadcast([P, CLUSTERS + EXPERTS + 5])).then_inc(sem("rows"), 16)
            sp.dma_start(squares, square_w).then_inc(sem("squares"), 16)
            sp.dma_start(cols[:, :], small_cols).then_inc(sem("cols"), 16)
            sp.dma_start(coarse_sb[:, :], coarse_w).then_inc(sem("coarse_w"), 16)
            sources = {"gate": gate_t, "up": up_t, "down": down_t}

            def weights(k):
                n, p0 = CHUNKS[k]
                part = k % RAW_PARTS
                if k >= RAW_PARTS:
                    sp.wait_ge(sem(f"split_lo{part}"), k // RAW_PARTS)
                sp.dma_start(raw[part], sources[n][:, p0:p0 + CHUNK, :]).then_inc(sem(f"raw{part}"), 16)

            sp.wait_ge(sem("gathered0"), 16 * TILES)
            for k in range(len(CHUNKS)):
                weights(k)
            store_gates(sp, 0)
            sequences(sp, lambda *a: sync_sequence(sp, *a))
            store(sp, BATCHES - 1)
            sp.wait_ge(sem("stored"), 16 * BATCHES + 16)
            sp.wait_ge(sem("gates_stored"), 16 * BATCHES)

        def pe_late(pe, b, par, p, early):
            f0, f1 = bank_f
            if p == PE_AT["xn_t"]:
                pe.wait_ge(sem("xn"), b + 1)
                wait(pe, "gates_t", b)
                for t in range(TILES):
                    last = pe.transpose(f0[:, t * P:t * P + P], xn[:, t, :], ident[:, :])
                last.then_inc(sem("pe_xn_t"), 1)
            if p == PE_AT["y"]:
                pe.wait_ge(sem("xn_hi"), b + 1)
                pe.wait_ge(sem("xn_lo"), b + 1)
                pe.matmul(f1[:, :], qk_hi[:, :], xn_hi[par][:, :], start=True, stop=False)
                pe.matmul(f1[:, :], qk_lo[:, :], xn_hi[par][:, :], start=False, stop=False)
                pe.matmul(f1[:, :], qk_hi[:, :], xn_lo[par][:, :], start=False, stop=True).then_inc(sem("pe_y"), 1)
            if p == PE_AT["z_scores"]:
                pe.wait_ge(sem("y_hi"), b + 1)
                pe.wait_ge(sem("y_lo"), b + 1)
                for t in range(TILES):
                    o = bank_f[t // 2][:, (t % 2) * 2 * P:(t % 2 + 1) * 2 * P]
                    c = slice(t * P, t * P + P)
                    hi, lo = (w[:, :].rearrange("p (k d) -> p k d", d=P)[:, 0:t + 2:t + 1, :] for w in (vo_y_hi, vo_y_lo))
                    pe.matmul(o, xn_hi[par][:, c], hi, start=(t % 2 == 0), stop=False, skip_group_check=True)
                    pe.matmul(o, xn_lo[par][:, c], hi, start=False, stop=False, skip_group_check=True)
                    last = pe.matmul(o, xn_hi[par][:, c], lo, start=False, stop=(t % 2 == 1), skip_group_check=True)
                last.then_inc(sem("pe_z_scores"), 1)
            if p == PE_AT["state"]:
                pe.wait_ge(sem("z"), 2 * b + 2)
                pe.wait_ge(sem("scores"), b + 1)
                pe.wait_ge(sem("xn_dec"), b + 1)
                for t in range(1, TILES):
                    last = pe.matmul(f0[:, (t - 1) * P:t * P], xn_dec[:, t - 1, :], z[:, t, :],
                                     start=(t == 1), stop=(t == TILES - 1), skip_group_check=True)
                last.then_inc(sem("pe_state"), 1)
            if p == PE_AT["mem"]:
                pe.wait_ge(sem("y_lo"), b + 1)
                pe.wait_ge(sem("state"), b + 1)
                for t in range(TILES):
                    last = pe.matmul(f1[:, t * P:t * P + P], scores[:, t, :], z[:, t, :],
                                     start=(t == 0), stop=(t == TILES - 1), skip_group_check=True)
                    if t < TILES - 1:
                        last = pe.matmul(f1[:, t * P:t * P + P], y_dec[:, t, :], state[:, t, :],
                                         start=False, stop=False, skip_group_check=True)
                last.then_inc(sem("pe_mem"), 1)
            if p == PE_AT["xn2_t"]:
                pe.wait_ge(sem("xn2"), b + 1)
                wait(pe, "result", b - 1)
                for t in range(TILES):
                    last = pe.transpose(f0[:, t * P:t * P + P], xn2[:, t, :], ident[:, :])
                last.then_inc(sem("pe_xn2_t"), 1)
            if p == PE_AT["vals"]:
                pe.wait_ge(sem("xn2_t"), b + 1)
                if early:
                    pe.wait_ge(sem("exp_t"), b + 2)
                pe.matmul(f1[:, :], read_mix[:, :], xn2_t[:, :], start=True, stop=True).then_inc(sem("pe_vals"), 1)
            if p == PE_AT["op"]:
                pe.wait_ge(sem("vals"), b + 1)
                if early:
                    pe.wait_ge(sem("h"), b + 2)
                for t in range(TILES):
                    last = pe.matmul(f0[:, t * P:t * P + P], vals[:, t * P:t * P + P], write_w[:, :],
                                     start=(t == 0), stop=(t == TILES - 1), skip_group_check=True)
                last.then_inc(sem("pe_op"), 1)
            if p == PE_AT["x3_t"]:
                pe.wait_ge(sem("x3"), b + 1)
                for t in range(TILES):
                    last = pe.transpose(f1[:, t * P:t * P + P], x3[:, t, :], ident[:, :])
                last.then_inc(sem("pe_x3_t"), 1)
            if p == PE_AT["router"]:
                pe.wait_ge(sem("x3_t"), b + 1)
                for t in range(TILES):
                    last = pe.matmul(f0[:, t * EXPERTS:(t + 1) * EXPERTS], x3_t[:, t * P:t * P + P], router_w[:, :],
                                     start=(t == 0), stop=(t == TILES - 1), skip_group_check=True)
                last.then_inc(sem("pe_router"), 1)
            if p == PE_AT["gates_t"]:
                pe.wait_ge(sem("gates"), b + 1)
                pe.wait_ge(sem("x3_lo"), b + 1)
                for t in range(TILES):
                    last = pe.transpose(f1[:, t * P:t * P + P], chosen_gates[:, t, :], ident[:, :])
                last.then_inc(sem("pe_gates_t"), 1)

        def pe_early(pe, b, p, banks=bank_f):
            f0, f1 = banks
            if p == PE_AT["exp_t"]:
                pe.wait_ge(sem("cluster_exp"), b + 1)
                wait(pe, "x2", b)
                alone(pe, "pe_passed")
                for t in range(TILES):
                    last = pe.transpose(f1[0:CLUSTERS, t * P:t * P + P], lg[:, t, :], ident[:, :])
                last.then_inc(sem("pe_exp_t"), 1)
            if p == PE_AT["coarse"]:
                pe.wait_ge(sem("exp_t"), b + 1)
                for t in range(TILES):
                    last = pe.matmul(f0[:, t * HALF:t * HALF + HALF], lge_t[:, t * P:t * P + P], coarse_sb[:, :],
                                     start=(t == 0), stop=(t == TILES - 1), skip_group_check=True)
                last.then_inc(sem("pe_coarse"), 1)

        def down(pe, b, par, p):
            q = PAIRS * b + p
            if isinstance(b, int) and b == 0 and p == 0:
                weights_split(pe, len(CHUNKS))
                pe.wait_ge(sem("h"), 2)
            pe.wait_ge(sem("hid_hi"), q + 1)
            pe.wait_ge(sem("hid_lo"), q + 1)
            s, y = slot(par, p), bank_y[par]
            pe.matmul(y[:, :], w_hi["down"][:, p, :], hid_hi[:, s, :], start=(p == 0), stop=False)
            pe.matmul(y[:, :], w_lo["down"][:, p, :], hid_hi[:, s, :], start=False, stop=False)
            pe.matmul(y[:, :], w_hi["down"][:, p, :], hid_lo[:, s, :], start=False,
                      stop=(p == PAIRS - 1)).then_inc(sem("down_done"), 1)

        def gate_up(pe, b, par, p):
            q = PAIRS * b + p
            ring = (p + par) % 2
            for name, banks, freed in (("gate", bank_g, "silu"), ("up", bank_u, "up_used")):
                wait(pe, freed, q - 1)
                o = banks[ring][:, :]
                pe.matmul(o, w_hi[name][:, p, :], x3_hi[par][:, :], start=True, stop=False)
                pe.matmul(o, w_lo[name][:, p, :], x3_hi[par][:, :], start=False, stop=False)
                pe.matmul(o, w_hi[name][:, p, :], x3_lo[par][:, :], start=False,
                          stop=True).then_inc(sem("pe_" + name), 1)

        def pe_out(pe, b):
            pe.wait_ge(sem("ffn_t"), b + 1)
            for t in range(TILES):
                last = pe.transpose(bank_f[0][:, t * P:t * P + P], ffn_t[:, t * P:t * P + P], ident[:, :])
            last.then_inc(sem("pe_out"), 1)

        def pe_sequence(pe, b, par, late, early, use=0):
            first = isinstance(b, int) and b == 0
            for p in range(PAIRS):
                if p >= AHEAD or not first:
                    gate_up(pe, b, par, p)
                if p >= LAG:
                    down(pe, b, par, p - LAG)
                elif not first:
                    down(pe, b - 1, 1 - par, p - LAG + PAIRS)
                if p == PE_AT["out"] and not first:
                    pe_out(pe, b - 1)
                if late:
                    pe_late(pe, b + 1, 1 - par, p, early)
                if early:
                    pe_early(pe, b + 2, p)

        @block.tensor
        def _(pe):
            f0, f1 = bank_f
            pe.wait_ge(sem("squares"), 16)
            pe.matmul(f0[:, 0:P], small_w["q"][:, :], small_w["k"][:, :], start=True, stop=True)
            pe.matmul(f0[:, P:2 * P], small_w["v"][:, :], small_w["o"][:, :], start=True, stop=True,
                      skip_group_check=True)
            pe.matmul(f0[:, 2 * P:3 * P], small_w["read"][:, :], basis[:, :], start=True, stop=True,
                      skip_group_check=True)
            pe.matmul(f0[:, 3 * P:4 * P], small_w["write"][:, :], basis[:, :], start=True, stop=True,
                      skip_group_check=True).then_inc(sem("pe_prep"), 1)
            pe.wait_ge(sem("ident"), 2)
            pe.wait_ge(sem("powers"), 3)
            pe.transpose(bank_g[0][:, 0:P], mask_t[:, :], ident[:, :])
            pe.matmul(bank_g[0][:, P:2 * P], to_end[:, :], ident[:, :], start=True, stop=True, skip_group_check=True)
            pe.matmul(bank_g[0][:, 2 * P:2 * P + 1], powers_t[:, :], ident[:, 0:1], start=True, stop=True,
                      skip_group_check=True).then_inc(sem("pe_powers"), 1)
            pe.wait_ge(sem("prep1"), 1)
            pe.matmul(f1[:, 0:P], qk_in[:, :], basis[:, :], start=True, stop=True)
            pe.matmul(f1[:, P:2 * P], vo_in[:, :], basis[:, :], start=True, stop=True,
                      skip_group_check=True).then_inc(sem("pe_prep"), 1)
            pe.wait_ge(sem("coarse_w"), 16)
            for p in range(PAIRS):
                pe_early(pe, 0, p, bank_y)
            pe.wait_ge(sem("prep2"), 1)
            pe.matmul(f0[:, 0:P], qk_t[:, :], basis[:, :], start=True, stop=True, skip_group_check=True)
            pe.matmul(f0[:, P:2 * P], vo_t[:, :], basis[:, :], start=True, stop=True, skip_group_check=True)
            pe.matmul(f0[:, 2 * P:3 * P], read_s[:, :], small_w["mix"][:, :], start=True, stop=True,
                      skip_group_check=True).then_inc(sem("pe_prep"), 1)
            pe.wait_ge(sem("prep3"), 1)
            pe.wait_ge(sem("cols"), 16)
            for p in range(PAIRS):
                if p == PE_AT["gates_t"]:
                    pe.wait_ge(sem("x3_hi"), 1)
                    pe.wait_ge(sem("x3_lo"), 1)
                    weights_split(pe, 2 * PAIRS // CHUNK)
                    for k in range(AHEAD):
                        gate_up(pe, 0, 0, k)
                pe_late(pe, 0, 0, p, False)
                pe_early(pe, 1, p - SHIFT, bank_y)
            sequences(pe, lambda *a: pe_sequence(pe, *a))
            last = BATCHES - 1
            for p in range(PAIRS - LAG, PAIRS):
                down(pe, last, 1, p)
            pe_out(pe, last)

        def act_late(act, b, par, p):
            f0, f1 = bank_f
            if p == ACT_AT["xn_hi"]:
                act.wait_ge(sem("pe_xn_t"), b + 1)
                act.activation(xn_hi[par][:, :], f0[:, :], ACT.Copy).then_inc(sem("xn_hi"), 1)
            if p == ACT_AT["y_hi"]:
                act.wait_ge(sem("pe_y"), b + 1)
                act.activation(vo_y_hi[:, P:], f1[:, :], ACT.Copy).then_inc(sem("y_hi"), 1)
            if p == ACT_AT["z"]:
                act.wait_ge(sem("pe_z_scores"), b + 1)
                for k in range(2):
                    act.activation(z[:, 2 * k:2 * k + 2, :], z_scores(k)[:, :, 0, :], ACT.Copy).then_inc(sem("z"), 1)
            if p in (ACT_AT["squares"], ACT_AT["squares2"]):
                first = 0 if p == ACT_AT["squares"] else TILES // 2
                act.wait_ge(sem("x2"), b + 1)
                for t in range(first, first + TILES // 2):
                    act.activation(x2_sq[:, t, :], x2[:, t, :], ACT.Square,
                                   accum_out=ss2[:, t:t + 1]).then_inc(sem("x2_squares"), 1)
            if p == ACT_AT["xn2_t"]:
                act.wait_ge(sem("pe_xn2_t"), b + 1)
                act.activation(xn2_t[:, :], f0[:, :], ACT.Copy).then_inc(sem("xn2_t"), 1)
            if p == ACT_AT["vals"]:
                act.wait_ge(sem("pe_vals"), b + 1)
                act.activation(vals[:, :], f1[:, :], ACT.Gelu, bias=bias_col[:, 0:1]).then_inc(sem("vals"), 1)
            if p == ACT_AT["x3_hi"]:
                act.wait_ge(sem("pe_x3_t"), b + 1)
                act.activation(x3_t[:, :], f1[:, :], ACT.Copy).then_inc(sem("x3_t"), 1)
                act.activation(x3_hi[par][:, :], f1[:, :], ACT.Copy).then_inc(sem("x3_hi"), 1)
            if p == ACT_AT["router_exp"]:
                act.wait_ge(sem("router_logits"), b + 1)
                act.activation(rl[:, :, :], rl[:, :, :], ACT.Exp).then_inc(sem("router_exp"), 1)

        def act_early(act, b, p, banks=bank_f):
            if p == ACT_AT["cluster_exp"]:
                act.wait_ge(sem("cluster_logits"), b + 1)
                act.activation(lg[:, :, :], lg[:, :, :], ACT.Exp).then_inc(sem("cluster_exp"), 1)
            if p == ACT_AT["exp_t"]:
                act.wait_ge(sem("pe_exp_t"), b + 1)
                act.activation(lge_t, banks[1][0:CLUSTERS, :], ACT.Copy).then_inc(sem("exp_t"), 1)

        def act_silu(act, b, par, p):
            q = PAIRS * b + p
            act.wait_ge(sem("pe_gate"), q + 1)
            if isinstance(b, int) and b == 0 and p == 0:
                weights_split(act, len(CHUNKS))
            wait(act, "hid_lo", q - RING + 1)
            act.activation(hid[:, slot(par, p), :], bank_g[(p + par) % 2][:, :], ACT.Silu).then_inc(sem("silu"), 1)

        def act_hi(act, b, par, p):
            q = PAIRS * b + p
            act.wait_ge(sem("gated"), q + 1)
            wait(act, "down_done", q - RING + 1)
            s = slot(par, p)
            act.activation(hid_hi[:, s, :], hid[:, s, :], ACT.Copy).then_inc(sem("hid_hi"), 1)

        def act_copy_out(act, b, par):
            act.wait_ge(sem("down_done"), PAIRS * b + PAIRS)
            act.activation(ffn_t, bank_y[par][:, :], ACT.Copy).then_inc(sem("ffn_t"), 1)

        def act_sequence(act, b, par, late, early, use=0):
            first = isinstance(b, int) and b == 0
            for p in range(PAIRS):
                if p == ACT_AT["ffn_t"] and not first:
                    act_copy_out(act, b - 1, 1 - par)
                if late:
                    act_late(act, b + 1, 1 - par, p)
                if early:
                    act_early(act, b + 2, p)
                act_silu(act, b, par, p)
                if p >= SPLIT_LAG:
                    act_hi(act, b, par, p - SPLIT_LAG)
                elif not first:
                    act_hi(act, b - 1, 1 - par, p - SPLIT_LAG + PAIRS)

        def split_hi(act, at):
            for k, (n, p0) in enumerate(CHUNKS):
                if HI_AT[k] == at:
                    part = k % RAW_PARTS
                    act.wait_ge(sem(f"raw{part}"), 16 * (k // RAW_PARTS + 1))
                    act.activation(w_hi[n][:, p0:p0 + CHUNK, :], raw[part], ACT.Copy).then_inc(sem("split_hi"), 1)

        @block.scalar
        def _(act):
            act.wait_ge(sem("rows"), 16)
            act.activation(sig[:, :], scalars[:, 0:1], ACT.Sigmoid).then_inc(sem("sigmoid"), 1)
            act.wait_ge(sem("read_shifted"), 1)
            act.activation(read_e[:, :], read_s[:, :], ACT.Exp, accum_out=read_stat[:, 1:2])\
               .then_inc(sem("read_exp"), 1)
            for p in range(PAIRS):
                act_early(act, 0, p, bank_y)
                split_hi(act, p - PAIRS)
            for p in range(PAIRS):
                act_late(act, 0, 0, p)
                act_early(act, 1, p - SHIFT, bank_y)
                split_hi(act, p)
            sequences(act, lambda *a: act_sequence(act, *a))
            last = BATCHES - 1
            for p in range(PAIRS - SPLIT_LAG, PAIRS):
                act_hi(act, last, 1, p)
            act_copy_out(act, last, 1)

        def dve_late(dve, b, par, p):
            f0, f1 = bank_f
            if p == DVE_AT["xn"]:
                dve.wait_ge(sem("inv1"), b + 1)
                for t in range(TILES):
                    last = dve.tensor_scalar(xn[:, t, :], emb[par][:, t, :], mv1[:, t, 0:1], inv1[:, 1, t:t + 1],
                                             ALU.subtract, ALU.mult)
                last.then_inc(sem("xn"), 1)
            if p == DVE_AT["x1"]:
                for t in range(TILES):
                    last = dve.tensor_scalar(x1[:, t, :], emb[par][:, t, :], mv1[:, t, 0:1], inv1[:, 0, t:t + 1],
                                             ALU.subtract, ALU.mult)
                last.then_inc(sem("x1"), 1)
            if p == DVE_AT["xn_dec"]:
                dve.wait_ge(sem("xn"), b + 1)
                dve.tensor_scalar(xn_dec[:, :, :], xn[:, 1:TILES, :], decay_cols[:, 0:1], None, ALU.mult)\
                   .then_inc(sem("xn_dec"), 1)
            if p == DVE_AT["xn_lo"]:
                dve.wait_ge(sem("xn_hi"), b + 1)
                dve.tensor_tensor(xn_lo[par][:, :], f0[:, :], xn_hi[par][:, :].bitcast(F32), ALU.subtract)\
                   .then_inc(sem("xn_lo"), 1)
            if p == DVE_AT["y_lo"]:
                dve.wait_ge(sem("y_hi"), b + 1)
                dve.tensor_tensor(vo_y_lo[:, P:], f1[:, :], vo_y_hi[:, P:].bitcast(F32), ALU.subtract)
                dve.tensor_tensor(y_dec[:, :, :], f1[:, 0:(TILES - 1) * P].rearrange("p (t d) -> p t d", d=P),
                                  decay_out[:, :].unsqueeze(1).to_broadcast([P, TILES - 1, P]), ALU.mult)\
                   .then_inc(sem("y_lo"), 1)
            if p == DVE_AT["scores"]:
                dve.wait_ge(sem("pe_z_scores"), b + 1)
                for k in range(2):
                    dve.wait_ge(sem("z"), 2 * b + k + 1)
                    last = dve.tensor_tensor(scores[:, 2 * k:2 * k + 2, :], z_scores(k)[:, :, 1, :],
                                             decay_mask[:, :].unsqueeze(1).to_broadcast([P, 2, P]), ALU.mult)
                last.then_inc(sem("scores"), 1)
            if p == DVE_AT["state"]:
                dve.wait_ge(sem("pe_state"), b + 1)
                dve.tensor_copy(state[:, TILES - 2, :], f0[:, (TILES - 2) * P:(TILES - 1) * P])\
                   .then_inc(sem("state_part"), 1)
                for k, c in enumerate(range(TILES - 3, -1, -1)):
                    dve.wait_ge(sem("state_part"), (TILES - 2) * b + k + 1)
                    dve.scalar_tensor_tensor(state[:, c, :], state[:, c + 1, :], decay_cols[:, 1:2],
                                             f0[:, c * P:c * P + P], ALU.mult, ALU.add)\
                       .then_inc(sem("state_part" if c else "state"), 1)
            if p == DVE_AT["x2"]:
                dve.wait_ge(sem("pe_mem"), b + 1)
                dve.wait_ge(sem("x1"), b + 1)
                dve.scalar_tensor_tensor(x2[:, :, :], tiles(f1), mem_mul[:, 0:1], x1[:, :, :], ALU.mult, ALU.add)\
                   .then_inc(sem("x2"), 1)
            if p == DVE_AT["xn2"]:
                dve.wait_ge(sem("inv2"), b + 1)
                for t in range(TILES):
                    last = dve.tensor_scalar(xn2[:, t, :], x2[:, t, :], inv2[:, t:t + 1], None, ALU.mult)
                last.then_inc(sem("xn2"), 1)
            if p == DVE_AT["h2"]:
                dve.wait_ge(sem("pe_op"), b + 1)
                dve.wait_ge(sem("hx"), b + 1)
                dve.scalar_tensor_tensor(h2[par][:, :, :], tiles(f0), op_mul[:, 0:1], hx[:, :, :], ALU.mult, ALU.add)\
                   .then_inc(sem("h2"), 1)
            if p == DVE_AT["bn3"]:
                dve.wait_ge(sem("h2"), b + 1)
                for t in range(TILES):
                    dve.bn_stats(bn3[:, t, :], h2[par][:, t, :]).then_inc(sem("bn3"), 1)
                dve.wait_ge(sem("bn3"), TILES * b + TILES)
                alone(dve, "dve_passed")
                for t in range(TILES):
                    last = dve.bn_aggr(mv3[:, t, :], bn3[:, t, :])
                last.then_inc(sem("mv3"), 1)
                dve.wait_ge(sem("mv3"), b + 1)
                dve.tensor_scalar(var3[:, :], mv3[:, :, 1], LN_EPS, None, ALU.add).then_inc(sem("var3"), 1)
            if p == DVE_AT["x3"]:
                dve.wait_ge(sem("inv3"), b + 1)
                for t in range(TILES):
                    last = dve.tensor_scalar(x3[:, t, :], h2[par][:, t, :], mv3[:, t, 0:1], inv3[:, t:t + 1],
                                             ALU.subtract, ALU.mult)
                last.then_inc(sem("x3"), 1)
            if p == DVE_AT["x3_lo"]:
                dve.wait_ge(sem("x3_hi"), b + 1)
                dve.tensor_tensor(x3_lo[par][:, :], f1[:, :], x3_hi[par][:, :].bitcast(F32), ALU.subtract)\
                   .then_inc(sem("x3_lo"), 1)
            if p == DVE_AT["router"]:
                dve.wait_ge(sem("pe_router"), b + 1)
                dve.tensor_tensor(rl[:, :, :], f0[:, 0:TILES * EXPERTS].rearrange("p (t e) -> p t e", t=TILES),
                                  router_b_row[:, :].unsqueeze(1).to_broadcast([P, TILES, EXPERTS]), ALU.add)\
                   .then_inc(sem("rl"), 1)
                dve.wait_ge(sem("rl"), b + 1)
                dve.tensor_reduce(rstat[:, 0, :], rl[:, :, :], AX.X, ALU.max).then_inc(sem("rl_max"), 1)
                dve.wait_ge(sem("rl_max"), b + 1)
                dve.tensor_tensor(rl[:, :, :], rl[:, :, :], over(rstat[:, 0, :], EXPERTS), ALU.subtract)\
                   .then_inc(sem("router_logits"), 1)
            if p == DVE_AT["prob"]:
                dve.wait_ge(sem("router_exp"), b + 1)
                dve.tensor_reduce(rstat[:, 1, :], rl[:, :, :], AX.X, ALU.add).then_inc(sem("re_sum"), 1)
                dve.wait_ge(sem("re_sum"), b + 1)
                dve.reciprocal(rstat[:, 2, :], rstat[:, 1, :]).then_inc(sem("re_inv"), 1)
                dve.wait_ge(sem("re_inv"), b + 1)
                dve.tensor_tensor(prob[:, :, 2:], rl[:, :, :], over(rstat[:, 2, :], EXPERTS), ALU.mult)\
                   .then_inc(sem("prob"), 1)
            if p == DVE_AT["top"]:
                dve.wait_ge(sem("prob"), b + 1)
                alone(dve, "dve_passed")
                for t in range(TILES):
                    dve.max(top8[:, t, :], prob[:, t, :]).then_inc(sem("top8"), 1)
                dve.wait_ge(sem("top8"), TILES * b + TILES)
                dve.tensor_reduce(tstat[:, 0, :], top8[:, :, 2:], AX.X, ALU.add).then_inc(sem("top_sum"), 1)
                dve.wait_ge(sem("top_sum"), b + 1)
                dve.tensor_scalar(tstat[:, 1, :], tstat[:, 0, :], GATE_EPS, None, ALU.add).then_inc(sem("top_eps"), 1)
            if p == DVE_AT["chosen"]:
                for t in range(TILES):
                    last = dve.match_replace(struck[:, t, :], top8[:, t, :], prob[:, t, :], -1.0)
                last.then_inc(sem("struck"), 1)
                dve.wait_ge(sem("struck"), b + 1)
                dve.tensor_scalar(chosen[:, :, :], struck[:, :, 2:], 0.0, None, ALU.is_lt).then_inc(sem("chosen"), 1)
                dve.wait_ge(sem("top_eps"), b + 1)
                dve.reciprocal(tstat[:, 2, :], tstat[:, 1, :]).then_inc(sem("top_inv"), 1)
            if p == DVE_AT["gates"]:
                dve.wait_ge(sem("top_inv"), b + 1)
                dve.tensor_tensor(gates[:, :, :], prob[:, :, 2:], over(tstat[:, 2, :], EXPERTS), ALU.mult)\
                   .then_inc(sem("gate_n"), 1)
                dve.wait_ge(sem("gate_n"), b + 1)
                dve.wait_ge(sem("chosen"), b + 1)
                dve.tensor_tensor(gates[:, :, :], gates[:, :, :], chosen[:, :, :], ALU.mult).then_inc(sem("gates"), 1)
            if p == DVE_AT["taken"]:
                first = isinstance(b, int) and b == 0
                if not first:
                    dve.wait_ge(sem("taken"), b)
                    dve.tensor_copy(taken_end[:, :], taken[:, SEQ - 1:SEQ]).then_inc(sem("taken_end"), 1)
                    dve.wait_ge(sem("taken_end"), b)
                dve.wait_ge(sem("pe_gates_t"), b + 1)
                dve.tensor_tensor_scan(taken[:, :], ones_row[:, :], f1[0:EXPERTS, :],
                                       0.0 if first else taken_end[:, :], ALU.mult, ALU.add)\
                   .then_inc(sem("taken"), 1)
                dve.wait_ge(sem("taken"), b + 1)
                wait(dve, "gates_stored", 16 * b)
                dve.scalar_tensor_tensor(gates_t[:, :], taken[:, :], float(CAPACITY), f1[EXPERTS:, :],
                                         ALU.is_le, ALU.mult).then_inc(sem("gates_t"), 1)

        def dve_early(dve, b, par, p, use, banks=bank_f):
            e = emb[par]
            if p == DVE_AT["logits"]:
                dve.wait_ge(sem(f"gathered{par}"), 16 * TILES * use)
                dve.tensor_tensor(lg[:, :, :], e[:, :, HALF:D],
                                  cluster_b_row[:, :].unsqueeze(1).to_broadcast([P, TILES, CLUSTERS]),
                                  ALU.add).then_inc(sem("lg"), 1)
                dve.wait_ge(sem("lg"), b + 1)
                dve.tensor_reduce(soft[:, 0, :], lg[:, :, :], AX.X, ALU.max).then_inc(sem("lg_max"), 1)
                dve.wait_ge(sem("lg_max"), b + 1)
                dve.tensor_tensor(lg[:, :, :], lg[:, :, :], over(soft[:, 0, :], CLUSTERS), ALU.subtract)\
                   .then_inc(sem("cluster_logits"), 1)
            if p == DVE_AT["exp_sum"]:
                dve.wait_ge(sem("cluster_exp"), b + 1)
                dve.tensor_reduce(soft[:, 1, :], lg[:, :, :], AX.X, ALU.add).then_inc(sem("lg_sum"), 1)
                dve.wait_ge(sem("lg_sum"), b + 1)
                dve.reciprocal(soft[:, 2, :], soft[:, 1, :]).then_inc(sem("lg_inv"), 1)
            if p == DVE_AT["h"]:
                dve.wait_ge(sem("pe_coarse"), b + 1)
                dve.wait_ge(sem("lg_inv"), b + 1)
                dve.tensor_tensor(e[:, :, HALF:D], banks[0][:, 0:TILES * HALF].rearrange("p (t d) -> p t d", t=TILES),
                                  over(soft[:, 2, :], HALF), ALU.mult).then_inc(sem("h"), 1)
            if p == DVE_AT["bn1"]:
                dve.wait_ge(sem("h"), b + 1)
                for t in range(TILES):
                    dve.bn_stats(bn1[:, t, :], e[:, t, :]).then_inc(sem("bn1"), 1)
            if p == DVE_AT["mv1"]:
                dve.wait_ge(sem("bn1"), TILES * b + TILES)
                alone(dve, "dve_passed")
                for t in range(TILES):
                    last = dve.bn_aggr(mv1[:, t, :], bn1[:, t, :])
                last.then_inc(sem("mv1"), 1)
                dve.wait_ge(sem("mv1"), b + 1)
                dve.tensor_scalar(var1[:, 0, :], mv1[:, :, 1], LN_EPS, None, ALU.add)
                dve.tensor_scalar(var1[:, 1, :], mv1[:, :, 1], 1.0 + RMS_EPS, RMS_EPS * LN_EPS, ALU.mult, ALU.add)\
                   .then_inc(sem("var1"), 1)

        def dve_up(dve, b, par, p):
            q = PAIRS * b + p
            dve.wait_ge(sem("silu"), q + 1)
            dve.wait_ge(sem("pe_up"), q + 1)
            s = slot(par, p)
            dve.tensor_tensor(hid[:, s, :], hid[:, s, :], bank_u[(p + par) % 2][:, :], ALU.mult)\
               .then_inc(sem("up_used"), 1)

        def dve_lo(dve, b, par, p):
            q = PAIRS * b + p
            dve.wait_ge(sem("hid_hi"), q + 1)
            s = slot(par, p)
            dve.tensor_tensor(hid_lo[:, s, :], hid[:, s, :], hid_hi[:, s, :].bitcast(F32), ALU.subtract)\
               .then_inc(sem("hid_lo"), 1)

        def dve_out(dve, b, par):
            dve.wait_ge(sem("pe_out"), b + 1)
            dve.wait_ge(sem("stored"), 16 * b + 16)
            dve.tensor_tensor(result[:, :, :], tiles(bank_f[0]), h2[par][:, :, :], ALU.add).then_inc(sem("result"), 1)

        def dve_sequence(dve, b, par, late, early, use=2):
            first = isinstance(b, int) and b == 0
            for p in range(PAIRS):
                if p == DVE_AT["result"] and not first:
                    dve_out(dve, b - 1, 1 - par)
                if late:
                    dve_late(dve, b + 1, 1 - par, p)
                if early:
                    dve_early(dve, b + 2, par, p, use)
                dve_up(dve, b, par, p)
                if p >= SPLIT_LAG:
                    dve_lo(dve, b, par, p - SPLIT_LAG)
                elif not first:
                    dve_lo(dve, b - 1, 1 - par, p - SPLIT_LAG + PAIRS)

        @block.vector
        def _(dve):
            dve.sem_inc(sem("stored"), 16)
            dve.memset(ones_row[:, :], 1.0).then_inc(sem("ones"), 1)
            dve.memset(ones[:, :], 1.0).then_inc(sem("ones"), 1)
            dve.memset(prob[:, :, 0:2], SENTINEL).then_inc(sem("sentinel"), 1)
            dve.wait_ge(sem("sigmoid"), 1)
            dve.wait_ge(sem("ones"), 2)
            dve.tensor_scalar(decay_full[:, :], ones[:, :], sig[:, 0:1], None, ALU.mult).then_inc(sem("decay_full"), 1)
            dve.wait_ge(sem("decay_full"), 1)
            dve.wait_ge(sem("above"), 2)
            dve.wait_ge(sem("ident"), 2)
            dve.tensor_tensor_scan(mask_t[:, :], decay_full[:, :], above[:, :], 0.0, ALU.mult, ALU.add)\
                .then_inc(sem("powers"), 1)
            dve.tensor_tensor_scan(powers_t[:, :], decay_full[:, :], ident[:, :], 0.0, ALU.mult, ALU.add)\
                .then_inc(sem("powers"), 1)
            dve.wait_ge(sem("powers"), 2)
            dve.tensor_scalar(to_end[:, :], ones[:, :], powers_t[:, P - 1:P], None, ALU.mult).then_inc(sem("powers"), 1)
            dve.wait_ge(sem("pe_prep"), 1)
            dve.tensor_reduce(read_stat[:, 0:1], bank_f[0][:, 2 * P:3 * P], AX.X, ALU.max).then_inc(sem("read_max"), 1)
            dve.tensor_copy(qk_in[:, :], bank_f[0][:, 0:P])
            dve.tensor_copy(vo_in[:, :], bank_f[0][:, P:2 * P])
            dve.tensor_copy(write_w[:, :], bank_f[0][:, 3 * P:4 * P]).then_inc(sem("prep1"), 1)
            dve.wait_ge(sem("read_max"), 1)
            dve.tensor_scalar(read_s[:, :], bank_f[0][:, 2 * P:3 * P], read_stat[:, 0:1], None, ALU.subtract)\
               .then_inc(sem("read_shifted"), 1)
            for p in range(PAIRS):
                dve_early(dve, 0, 0, p, 1, bank_y)
                if p == DVE_AT["logits"]:
                    dve.wait_ge(sem("pe_prep"), 2)
                    dve.tensor_copy(qk_t[:, :], bank_f[1][:, 0:P])
                    dve.tensor_copy(vo_t[:, :], bank_f[1][:, P:2 * P])
                    dve.wait_ge(sem("read_exp"), 1)
                    dve.reciprocal(read_stat[:, 2:3], read_stat[:, 1:2]).then_inc(sem("read_inv"), 1)
                    dve.wait_ge(sem("read_inv"), 1)
                    dve.tensor_scalar(read_s[:, :], read_e[:, :], read_stat[:, 2:3], None, ALU.mult).then_inc(sem("prep2"), 1)
                if p == DVE_AT["mv1"]:
                    dve.wait_ge(sem("pe_prep"), 3)
                    dve.tensor_copy(qk_hi[:, :], bank_f[0][:, 0:P])
                    dve.tensor_copy(vo_y_hi[:, 0:P], bank_f[0][:, P:2 * P]).then_inc(sem("weights_hi"), 1)
                    dve.wait_ge(sem("weights_hi"), 1)
                    dve.tensor_tensor(qk_lo[:, :], bank_f[0][:, 0:P], qk_hi[:, :].bitcast(F32), ALU.subtract)
                    dve.tensor_tensor(vo_y_lo[:, 0:P], bank_f[0][:, P:2 * P], vo_y_hi[:, 0:P].bitcast(F32), ALU.subtract)
                    dve.tensor_copy(read_mix[:, :], bank_f[0][:, 2 * P:3 * P]).then_inc(sem("prep3"), 1)
                    dve.wait_ge(sem("rows"), 16)
                    dve.tensor_tensor(mem_mul[:, :], scalars[:, 1:2], scalars[:, 3:4], ALU.mult).then_inc(sem("muls"), 1)
                    dve.tensor_tensor(op_mul[:, :], scalars[:, 2:3], scalars[:, 4:5], ALU.mult).then_inc(sem("muls"), 1)
                    dve.wait_ge(sem("sentinel"), 1)
                    dve.wait_ge(sem("muls"), 2)
                    dve.wait_ge(sem("pe_powers"), 1)
                    dve.tensor_copy(decay_mask[:, :], bank_g[0][:, 0:P])
                    dve.tensor_copy(decay_out[:, :], bank_g[0][:, P:2 * P]).then_inc(sem("decays"), 1)
                    dve.tensor_copy(decay_cols[:, 0:1], bank_g[0][:, 2 * P:2 * P + 1]).then_inc(sem("decays"), 1)
                    dve.wait_ge(sem("decays"), 2)
                    dve.tensor_tensor(decay_cols[:, 1:2], decay_out[:, 0:1], decay_full[:, 0:1], ALU.mult)\
                        .then_inc(sem("decays"), 1)
                split_lo(dve, "vector", p - PAIRS)
            dve.wait_ge(sem("decays"), 3)
            for p in range(PAIRS):
                dve_late(dve, 0, 0, p)
                dve_early(dve, 1, 1, p - SHIFT, 1, bank_y)
                split_lo(dve, "vector", p)
            sequences(dve, lambda *a: dve_sequence(dve, *a))
            last = BATCHES - 1
            for p in range(PAIRS - SPLIT_LAG, PAIRS):
                dve_lo(dve, last, 1, p)
            dve_out(dve, last, 1)

        def gather(pool, b, par, t, prev_use):
            if isinstance(b, int):
                at = idx[:, b * TILES + t:b * TILES + t + 1]
            else:
                at = idx_now[:, t:t + 1]
            if t == 0:
                wait(pool, "hx", b - 1)
                if not isinstance(b, int):
                    pool.wait_ge(sem(f"gathered{1 - par}"), 16 * TILES * prev_use)
                    pool.tensor_copy(idx_now[:, :], idx[:, bass.ds(b * TILES, TILES)]).then_inc(sem("idx_now"), 1)
                    pool.wait_ge(sem("idx_now"), b - 2)
                alone(pool, "pool_passed")
            pool.indirect_dma_start(emb[par][:, t, :], None, table[:, :],
                                    bass.IndirectOffsetOnAxis(ap=at, axis=0)).then_inc(sem(f"gathered{par}"), 16)

        def pool_late(pool, b, par, p):
            if p == POOL_AT["inv2"]:
                pool.wait_ge(sem("x2_squares"), TILES * b + TILES)
                alone(pool, "pool_passed")
                pool.tensor_scalar(ms2[:, :], ss2[:, :], 1.0 / D, RMS_EPS, ALU.mult, ALU.add).then_inc(sem("ms2"), 1)
                pool.wait_ge(sem("ms2"), b + 1)
                pool.tensor_tensor(inv2[:, :], ms2[:, :], neg_half[:, 0:TILES], ALU.pow).then_inc(sem("inv2"), 1)
            if p == POOL_AT["hx"]:
                pool.wait_ge(sem("x2"), b + 1)
                pool.tensor_tensor(hx[:, :, :], emb[par][:, :, :], x2[:, :, :], ALU.add).then_inc(sem("hx"), 1)
            if p == POOL_AT["inv3"]:
                pool.wait_ge(sem("var3"), b + 1)
                pool.tensor_tensor(inv3[:, :], var3[:, :], neg_half[:, 0:TILES], ALU.pow).then_inc(sem("inv3"), 1)

        def pool_early(pool, b, p):
            if p == POOL_AT["inv1"]:
                pool.wait_ge(sem("var1"), b + 1)
                pool.tensor_tensor(inv1[:, :, :], var1[:, :, :], neg_half[:, :].rearrange("p (k t) -> p k t", k=2),
                                   ALU.pow).then_inc(sem("inv1"), 1)

        def pool_sequence(pool, b, par, late, early, use=0):
            for p in range(PAIRS):
                if late:
                    pool_late(pool, b + 1, 1 - par, p)
                if early:
                    pool_early(pool, b + 2, p)
                    if p in GATHER_AT:
                        gather(pool, b + 2, par, GATHER_AT.index(p), use if par else use - 1)
                q = PAIRS * b + p
                s = slot(par, p)
                pool.wait_ge(sem("up_used"), q + 1)
                if p:
                    row, uses = (p - 1) % GATE_RING, ROUTED_PAIRS // GATE_RING
                    pool.wait_ge(sem(f"gate_rows{row}"), 16 * uses * b + 16 * ((p - 1) // GATE_RING + 1))
                    pool.tensor_tensor(hid[:, s, :], hid[:, s, :], gate_rows[:, row, :], ALU.mult)\
                        .then_inc(sem("gated"), 1)
                else:
                    alone(pool, "pool_passed")
                    pool.tensor_scalar(hid[:, s, :], hid[:, s, :], 1.0 / SHARED, None, ALU.mult)\
                        .then_inc(sem("gated"), 1)

        @block.gpsimd
        def _(pool):
            pool.memset(ident[:, :], 0.0).then_inc(sem("ident"), 1)
            pool.wait_ge(sem("ident"), 1)
            pool.affine_select(out=ident[:, :], in_=ident[:, :], compare_op=ALU.not_equal, fill=1.0,
                               base=0, pattern=[[-1, P]], channel_multiplier=1).then_inc(sem("ident"), 1)
            pool.memset(neg_half[:, :], -0.5).then_inc(sem("halves"), 1)
            pool.memset(above[:, :], 0.0).then_inc(sem("above"), 1)
            pool.wait_ge(sem("above"), 1)
            pool.affine_select(out=above[:, :], in_=above[:, :], compare_op=ALU.not_equal, fill=1.0,
                               base=1, pattern=[[-1, P]], channel_multiplier=1).then_inc(sem("above"), 1)
            pool.wait_ge(sem("idx"), 16)
            for t in range(TILES):
                gather(pool, 0, 0, t, 0)
            pool.wait_ge(sem("halves"), 1)
            for t in range(TILES):
                gather(pool, 1, 1, t, 0)
            for p in range(PAIRS):
                pool_early(pool, 0, p)
                split_lo(pool, "pool", p - PAIRS)
            for p in range(PAIRS):
                pool_late(pool, 0, 0, p)
                pool_early(pool, 1, p - SHIFT)
                split_lo(pool, "pool", p)
            sequences(pool, lambda *a: pool_sequence(pool, *a))


def kernel(x, L0_tok_fine_embed_w, L0_tok_coarse_embed_w, L0_tok_loc_to_cluster_w, L0_tok_loc_to_cluster_b,
           L0_attn_basis, L0_attn_q_coeffs, L0_attn_k_coeffs, L0_attn_v_coeffs, L0_attn_o_coeffs,
           L0_attn_decay_logit, L0_attn_mem_out_scale, L0_attn_read_coeffs, L0_attn_write_coeffs,
           L0_attn_channel_mix, L0_attn_bias, L0_attn_op_out_scale, L0_attn_mem_scale, L0_attn_op_scale,
           L0_ffn_router_w, L0_ffn_bias, L0_ffn_shared_w_gate, L0_ffn_shared_w_up, L0_ffn_shared_w_down,
           L0_ffn_w_gate, L0_ffn_w_up, L0_ffn_w_down):
    import numpy as np
    import concourse.bacc as bacc
    from concourse.bass_utils import run_bass_kernel_spmd as run

    def a(v):
        return np.asarray(v)

    def in_rows(routed, shared):
        both = np.concatenate([a(shared), a(routed)], axis=0)
        return both.transpose(2, 0, 1).reshape(D, PAIRS, 2 * F)

    def down_rows(routed, shared):
        both = np.concatenate([a(shared), a(routed)], axis=0)
        return both.reshape(PAIRS, 2, D, F).transpose(1, 3, 0, 2).reshape(2 * F, PAIRS, D)

    laid_out = {
        "ids": a(x).reshape(BATCHES * TILES, P).T,
        "table": np.concatenate([a(L0_tok_fine_embed_w), a(L0_tok_loc_to_cluster_w).T], axis=1),
        "coarse_w": a(L0_tok_coarse_embed_w),
        "square_w": np.concatenate([
            a(L0_attn_basis).T, a(L0_attn_q_coeffs), a(L0_attn_k_coeffs), a(L0_attn_v_coeffs), a(L0_attn_o_coeffs),
            a(L0_attn_read_coeffs).T, a(L0_attn_write_coeffs).T, a(L0_attn_channel_mix)], axis=1),
        "small_cols": np.concatenate([a(L0_ffn_router_w).T, a(L0_attn_bias).reshape(C, 1)], axis=1),
        "small_rows": np.concatenate([
            a(v).reshape(1, -1) for v in (L0_tok_loc_to_cluster_b, L0_ffn_bias, L0_attn_decay_logit,
                                          L0_attn_mem_out_scale, L0_attn_op_out_scale, L0_attn_mem_scale,
                                          L0_attn_op_scale)], axis=1),
        "gate_t": in_rows(L0_ffn_w_gate, L0_ffn_shared_w_gate),
        "up_t": in_rows(L0_ffn_w_up, L0_ffn_shared_w_up),
        "down_t": down_rows(L0_ffn_w_down, L0_ffn_shared_w_down),
    }
    nc = bacc.Bacc("TRN2", target_bir_lowering=False, num_devices=1)
    arrays, args = {}, []
    for name, v in laid_out.items():
        v = np.ascontiguousarray(v)
        arrays[name + "_dram"] = v
        args.append(nc.dram_tensor(name + "_dram", v.shape, mybir.dt.from_np(v.dtype), kind="ExternalInput").ap())
    args.append(nc.dram_tensor("out_dram", (BATCHES, SEQ, D), F32, kind="ExternalOutput").ap())
    build(nc, *args)
    return run(nc, [arrays], core_ids=[0]).results[0]["out_dram"]
```
